# Optimizing a Trainium2 kernel written in Bass

```python
import numpy as np
import jax
import jax.numpy as jnp

def _softmax(x, axis=-1):
    return jax.nn.softmax(x, axis=axis)

def _gelu(x):
    return jax.nn.gelu(x, approximate=True)

def _silu(x):
    return jax.nn.silu(x)

def _sigmoid(x):
    return jax.nn.sigmoid(x)

def _layernorm(x, axis=-1, eps=1e-05):
    m = jnp.mean(x, axis=axis, keepdims=True)
    v = jnp.var(x, axis=axis, keepdims=True)
    return (x - m) / jnp.sqrt(v + eps)

def _scatter_add(tgt, idx, src, axis=0):
    return tgt.at[idx].add(src)

def _segment_sum(src, seg, n):
    return jax.ops.segment_sum(src, seg, n)
kernel_name = 'mk_macaron_d2_jaxref_r8_bb349e'

def setup_inputs(seed: int=0):
    np.random.seed(seed)
    _w = jnp.asarray

    def _L0_attn_setup():
        import jax, jax.numpy as jnp
        import numpy as np
        import math
        IN_DIM = 128
        LATENT_DIM = 32
        OUT_DIM = 128

        def _kaiming(key, fan_out, fan_in):
            std = math.sqrt(2.0 / fan_in)
            return jax.random.normal(key, (fan_out, fan_in), dtype=jnp.float32) * std
        key = jax.random.key(seed)
        kx, kt, kp, kg = jax.random.split(key, 4)
        x = jax.random.normal(kx, (8, 512, IN_DIM), dtype=jnp.float32)
        W_theta = _kaiming(kt, LATENT_DIM, IN_DIM)
        W_phi = _kaiming(kp, LATENT_DIM, IN_DIM)
        W_g = _kaiming(kg, OUT_DIM, IN_DIM)
        return {'x': x, 'W_theta': W_theta, 'W_phi': W_phi, 'W_g': W_g}
    _L0_attn_in = _L0_attn_setup()

    def _L0_ffn_setup():
        import jax, jax.numpy as jnp
        import numpy as np
        D_IN, D_HID = (128, 512)

        def _ternary(key, shape):
            return jax.random.randint(key, shape, -1, 2).astype(jnp.float32)

        def _tlin(x, w, s):
            return jnp.einsum('bsi,oi->bso', x, w) * s
        key = jax.random.key(seed)
        ks = jax.random.split(key, 12)
        inv = lambda fan: 1.0 / np.sqrt(fan).astype(np.float32)
        return {'x': jax.random.normal(ks[0], (4, 256, D_IN), dtype=jnp.float32), 'w1_w': _ternary(ks[1], (D_HID, D_IN)), 'w1_s': jax.random.uniform(ks[2], (D_HID,), dtype=jnp.float32) * inv(D_IN), 'w2_w': _ternary(ks[3], (D_HID, D_IN)), 'w2_s': jax.random.uniform(ks[4], (D_HID,), dtype=jnp.float32) * inv(D_IN), 'h1_w': _ternary(ks[5], (D_HID, D_HID)), 'h1_s': jax.random.uniform(ks[6], (D_HID,), dtype=jnp.float32) * inv(D_HID), 'h2_w': _ternary(ks[7], (D_HID, D_HID)), 'h2_s': jax.random.uniform(ks[8], (D_HID,), dtype=jnp.float32) * inv(D_HID), 'w3_w': _ternary(ks[9], (D_IN, D_HID)), 'w3_s': jax.random.uniform(ks[10], (D_IN,), dtype=jnp.float32) * inv(D_HID)}
    _L0_ffn_in = _L0_ffn_setup()

    def _L1_attn_setup():
        import jax, jax.numpy as jnp
        import numpy as np
        NUM_HEADS = 16
        THETA = 10000.0

        def _rope(x, theta):
            S, d_k = (x.shape[1], x.shape[-1])
            k = jnp.arange(d_k // 2, dtype=jnp.float32)
            inv_freq = theta ** (-2.0 * k / d_k)
            ang = jnp.arange(S, dtype=jnp.float32)[:, None] * inv_freq
            cos = jnp.cos(ang)[None, :, None, :]
            sin = jnp.sin(ang)[None, :, None, :]
            x_even = x[..., 0::2]
            x_odd = x[..., 1::2]
            y_even = cos * x_even - sin * x_odd
            y_odd = sin * x_even + cos * x_odd
            y = jnp.stack([y_even, y_odd], axis=-1)
            return y.reshape(x.shape)
        key = jax.random.key(seed)
        ks = jax.random.split(key, 5)
        B, S, D = (2, 256, 128)
        std = 1.0 / np.sqrt(D)
        return {'in_features': jax.random.normal(ks[0], (B, S, D), dtype=jnp.float32), 'W_Q': jax.random.normal(ks[1], (D, D), dtype=jnp.float32) * std, 'W_K': jax.random.normal(ks[2], (D, D), dtype=jnp.float32) * std, 'W_V': jax.random.normal(ks[3], (D, D), dtype=jnp.float32) * std, 'W_O': jax.random.normal(ks[4], (D, D), dtype=jnp.float32) * std}
    _L1_attn_in = _L1_attn_setup()

    def _L1_ffn_setup():
        import jax, jax.numpy as jnp
        import numpy as np
        B, L, H = (8, 256, 128)
        E, K, R = (8, 2, 64)

        def _gates(cls_tok, Wr):
            logits = cls_tok @ Wr.T
            top_vals, top_idx = jax.lax.top_k(logits, K)
            neg_inf = jnp.full_like(logits, -jnp.inf)
            rows = jnp.arange(logits.shape[0])[:, None]
            masked = neg_inf.at[rows, top_idx].set(top_vals)
            return jax.nn.softmax(masked, axis=-1)
        key = jax.random.key(seed)
        k1, k2, k3, k4 = jax.random.split(key, 4)
        x = jax.random.normal(k1, (B, L, H), dtype=jnp.float32)
        Wr = jax.random.normal(k2, (E, H), dtype=jnp.float32) * (1.0 / np.sqrt(H))
        A = jax.random.normal(k3, (E, R, H), dtype=jnp.float32) * (1.0 / np.sqrt(H))
        Bw = jax.random.normal(k4, (E, H, R), dtype=jnp.float32) * (1.0 / np.sqrt(R))
        return {'x': x, 'Wr': Wr, 'A': A, 'Bw': Bw}
    _L1_ffn_in = _L1_ffn_setup()
    _d = {'L0_attn_x': _L0_attn_in['x'], 'L0_attn_W_theta': _L0_attn_in['W_theta'], 'L0_attn_W_phi': _L0_attn_in['W_phi'], 'L0_attn_W_g': _L0_attn_in['W_g'], 'L0_ffn_w1_w': _L0_ffn_in['w1_w'], 'L0_ffn_w1_s': _L0_ffn_in['w1_s'], 'L0_ffn_w2_w': _L0_ffn_in['w2_w'], 'L0_ffn_w2_s': _L0_ffn_in['w2_s'], 'L0_ffn_h1_w': _L0_ffn_in['h1_w'], 'L0_ffn_h1_s': _L0_ffn_in['h1_s'], 'L0_ffn_h2_w': _L0_ffn_in['h2_w'], 'L0_ffn_h2_s': _L0_ffn_in['h2_s'], 'L0_ffn_w3_w': _L0_ffn_in['w3_w'], 'L0_ffn_w3_s': _L0_ffn_in['w3_s'], 'L1_attn_W_Q': _L1_attn_in['W_Q'], 'L1_attn_W_K': _L1_attn_in['W_K'], 'L1_attn_W_V': _L1_attn_in['W_V'], 'L1_attn_W_O': _L1_attn_in['W_O'], 'L1_ffn_Wr': _L1_ffn_in['Wr'], 'L1_ffn_A': _L1_ffn_in['A'], 'L1_ffn_Bw': _L1_ffn_in['Bw']}
    _x0 = _d['L0_attn_x']
    _d['L0_attn_x'] = jax.random.normal(jax.random.fold_in(jax.random.key(seed), 1), (16, 256, 128), dtype=_x0.dtype)
    del _x0
    return _d

def reference(L0_attn_x, L0_attn_W_theta, L0_attn_W_phi, L0_attn_W_g, L0_ffn_w1_w, L0_ffn_w1_s, L0_ffn_w2_w, L0_ffn_w2_s, L0_ffn_h1_w, L0_ffn_h1_s, L0_ffn_h2_w, L0_ffn_h2_s, L0_ffn_w3_w, L0_ffn_w3_s, L1_attn_W_Q, L1_attn_W_K, L1_attn_W_V, L1_attn_W_O, L1_ffn_Wr, L1_ffn_A, L1_ffn_Bw):

    def _L0_attn_ref(x, W_theta, W_phi, W_g):
        import jax, jax.numpy as jnp
        import numpy as np
        import math
        IN_DIM = 128
        LATENT_DIM = 32
        OUT_DIM = 128

        def _kaiming(key, fan_out, fan_in):
            std = math.sqrt(2.0 / fan_in)
            return jax.random.normal(key, (fan_out, fan_in), dtype=jnp.float32) * std
        theta_x = jnp.einsum('bnf,lf->bnl', x, W_theta)
        phi_x = jnp.einsum('bnf,lf->bnl', x, W_phi)
        fun_g_x = jnp.einsum('bnf,of->bno', x, W_g)
        scale = 1.0 / math.sqrt(IN_DIM)
        att = jnp.einsum('bnl,bml->bnm', theta_x, phi_x) * scale
        return jnp.einsum('bnm,bmo->bno', att, fun_g_x)

    def _L0_ffn_ref(x, w1_w, w1_s, w2_w, w2_s, h1_w, h1_s, h2_w, h2_s, w3_w, w3_s):
        import jax, jax.numpy as jnp
        import numpy as np
        D_IN, D_HID = (128, 512)

        def _ternary(key, shape):
            return jax.random.randint(key, shape, -1, 2).astype(jnp.float32)

        def _tlin(x, w, s):
            return jnp.einsum('bsi,oi->bso', x, w) * s
        h = jax.nn.silu(_tlin(x, w1_w, w1_s)) * _tlin(x, w2_w, w2_s)
        h = jax.nn.gelu(_tlin(h, h1_w, h1_s), approximate=False)
        h = jax.nn.gelu(_tlin(h, h2_w, h2_s), approximate=False)
        return _tlin(h, w3_w, w3_s)

    def _L1_attn_ref(in_features, W_Q, W_K, W_V, W_O):
        import jax, jax.numpy as jnp
        import numpy as np
        NUM_HEADS = 16
        THETA = 10000.0

        def _rope(x, theta):
            S, d_k = (x.shape[1], x.shape[-1])
            k = jnp.arange(d_k // 2, dtype=jnp.float32)
            inv_freq = theta ** (-2.0 * k / d_k)
            ang = jnp.arange(S, dtype=jnp.float32)[:, None] * inv_freq
            cos = jnp.cos(ang)[None, :, None, :]
            sin = jnp.sin(ang)[None, :, None, :]
            x_even = x[..., 0::2]
            x_odd = x[..., 1::2]
            y_even = cos * x_even - sin * x_odd
            y_odd = sin * x_even + cos * x_odd
            y = jnp.stack([y_even, y_odd], axis=-1)
            return y.reshape(x.shape)
        B, S, D = in_features.shape
        H = NUM_HEADS
        d_k = D // H
        scale = 1.0 / np.sqrt(np.float32(d_k))
        q = jnp.einsum('kd,bsd->bsk', W_Q, in_features).reshape(B, S, H, d_k)
        k = jnp.einsum('kd,bsd->bsk', W_K, in_features).reshape(B, S, H, d_k)
        v = jnp.einsum('vd,bsd->bsv', W_V, in_features).reshape(B, S, H, d_k)
        q = _rope(q, THETA)
        k = _rope(k, THETA)
        q = q.transpose(0, 2, 1, 3)
        k = k.transpose(0, 2, 1, 3)
        v = v.transpose(0, 2, 1, 3)
        scores = jnp.einsum('bhqd,bhkd->bhqk', q, k) * scale
        causal = jnp.tril(jnp.ones((S, S), dtype=bool))
        scores = jnp.where(causal[None, None], scores, -jnp.inf)
        attn = jax.nn.softmax(scores, axis=-1)
        out = jnp.einsum('bhqk,bhkd->bhqd', attn, v)
        out = out.transpose(0, 2, 1, 3).reshape(B, S, D)
        return jnp.einsum('dv,bsv->bsd', W_O, out)

    def _L1_ffn_ref(x, Wr, A, Bw):
        import jax, jax.numpy as jnp
        import numpy as np
        B, L, H = (8, 256, 128)
        E, K, R = (8, 2, 64)

        def _gates(cls_tok, Wr):
            logits = cls_tok @ Wr.T
            top_vals, top_idx = jax.lax.top_k(logits, K)
            neg_inf = jnp.full_like(logits, -jnp.inf)
            rows = jnp.arange(logits.shape[0])[:, None]
            masked = neg_inf.at[rows, top_idx].set(top_vals)
            return jax.nn.softmax(masked, axis=-1)
        gates = _gates(x[:, 0, :], Wr)
        mid = jnp.einsum('blh,erh->belr', x, A)
        expert_out = jnp.einsum('belr,ehr->belh', mid, Bw)
        weighted = jnp.einsum('be,belh->blh', gates, expert_out)
        return x + weighted
    x = L0_attn_x
    x = x + 0.5 * _L0_ffn_ref(_layernorm(x, axis=-1), L0_ffn_w1_w, L0_ffn_w1_s, L0_ffn_w2_w, L0_ffn_w2_s, L0_ffn_h1_w, L0_ffn_h1_s, L0_ffn_h2_w, L0_ffn_h2_s, L0_ffn_w3_w, L0_ffn_w3_s)
    x = x + _L0_attn_ref(_layernorm(x, axis=-1), L0_attn_W_theta, L0_attn_W_phi, L0_attn_W_g)
    x = x + 0.5 * _L0_ffn_ref(_layernorm(x, axis=-1), L0_ffn_w1_w, L0_ffn_w1_s, L0_ffn_w2_w, L0_ffn_w2_s, L0_ffn_h1_w, L0_ffn_h1_s, L0_ffn_h2_w, L0_ffn_h2_s, L0_ffn_w3_w, L0_ffn_w3_s)
    x = x + 0.5 * _L1_ffn_ref(_layernorm(x, axis=-1), L1_ffn_Wr, L1_ffn_A, L1_ffn_Bw)
    x = x + _L1_attn_ref(_layernorm(x, axis=-1), L1_attn_W_Q, L1_attn_W_K, L1_attn_W_V, L1_attn_W_O)
    x = x + 0.5 * _L1_ffn_ref(_layernorm(x, axis=-1), L1_ffn_Wr, L1_ffn_A, L1_ffn_Bw)
    return x

_drawn_inputs = setup_inputs


def setup_inputs(seed=0):
    import zlib

    import numpy as np

    out = dict(_drawn_inputs(seed))
    spreads = {}
    factors = {}
    for name, (base, spread) in spreads.items():
        noise = np.random.default_rng([zlib.crc32(name.encode()), seed]).standard_normal(out[name].shape)
        drawn = base * np.exp(spread * noise) if base else spread * noise
        out[name] = jnp.asarray(drawn.astype(out[name].dtype))
    for name, factor in factors.items():
        out[name] = (out[name] * factor).astype(out[name].dtype)
    return out
```

```python
from contextlib import ExitStack

import numpy as np
import concourse.bass as bass
from concourse import mybir

F32 = mybir.dt.float32
F32R = mybir.dt.float32r
BF16 = mybir.dt.bfloat16
ALU = mybir.AluOpType
ACT = mybir.ActivationFunctionType
AX = mybir.AxisListType.X

NB = 16
S = 256
D = 128
HID = 512
NC = 8
TC = 512
NH = 16
DK = 8
EPS = 1e-5
NEG = -1.0e30
LEAD = 7


def activation(*a, **k):
    return lambda e: e.activation(*a, **k)


def affine_select(*a, **k):
    return lambda e: e.affine_select(*a, **k)


def bn_aggr(*a, **k):
    return lambda e: e.bn_aggr(*a, **k)


def bn_stats(*a, **k):
    return lambda e: e.bn_stats(*a, **k)


def matmul(*a, **k):
    return lambda e: e.matmul(*a, **k)


def memset(*a, **k):
    return lambda e: e.memset(*a, **k)


def reciprocal(*a, **k):
    return lambda e: e.reciprocal(*a, **k)


def reduce_max(*a, **k):
    return lambda e: e.reduce_max(*a, **k)


def scalar_tensor_tensor(*a, **k):
    return lambda e: e.scalar_tensor_tensor(*a, **k)


def tensor_copy(*a, **k):
    return lambda e: e.tensor_copy(*a, **k)


def tensor_reduce(*a, **k):
    return lambda e: e.tensor_reduce(*a, **k)


def tensor_scalar(*a, **k):
    return lambda e: e.tensor_scalar(*a, **k)


def tensor_tensor(*a, **k):
    return lambda e: e.tensor_tensor(*a, **k)


def transpose(*a, **k):
    return lambda e: e.transpose(*a, **k)


class Tok:
    def __init__(self, sem, val):
        self.sem, self.val = sem, val


class Queue:

    def __init__(self, sem):
        self.sem, self.n, self.ops = sem, 0, []

    def put(self, fn, waits=(), lo=False, inc=True):
        tok = None
        if inc:
            self.n += 1
            tok = Tok(self.sem, self.n)
        self.ops.append((fn, [w for w in waits if w is not None], inc, lo))
        return tok

    def play(self, eng, lo=True):
        seen = {}
        for fn, waits, inc, is_lo in self.ops:
            for w in waits:
                if seen.get(id(w.sem), 0) < w.val:
                    eng.wait_ge(w.sem, w.val)
                    seen[id(w.sem)] = w.val
            if is_lo and not lo:
                continue
            ins = fn(eng)
            if inc:
                ins.then_inc(self.sem, 1)


class Ring:

    def __init__(self, n):
        self.n, self.i, self.free = n, -1, [[] for _ in range(n)]

    def take(self):
        self.i += 1
        return self.i % self.n, self.free[self.i % self.n]


def staggered(tasks, lag):
    live, n, tick = [], 0, 0
    tasks = list(tasks)
    while n < len(tasks) or live:
        if n < len(tasks) and tick % lag == 0:
            live.append(tasks[n])
            n += 1
        for t in list(live):
            if next(t, "end") == "end":
                live.remove(t)
        tick += 1


def build(nc, I, out):
    with ExitStack() as ctx:
        def sb(name, shape, dt=F32):
            return ctx.enter_context(nc.sbuf_tensor(name, shape, dt))

        def sem(name):
            return ctx.enter_context(nc.semaphore(name))

        X = sb("X", [128, 32, D])
        IDN = sb("IDN", [128, 128])
        HIDN = sb("HIDN", [128, 128])
        IDB = sb("IDB", [128, 128], BF16)
        MKB = sb("MKB", [128, 512], BF16)
        SC = sb("SC", [128, 17])
        TH = sb("TH", [128, 32])
        PG = sb("PG", [128, 160])
        WR = sb("WR", [128, 8])
        AE = sb("AE", [128, 4, 128])
        BT = sb("BT", [128, 4, 128])
        WQ = sb("WQ", [128, 5, 128])
        WO = sb("WO", [128, 128])
        TRI = sb("TRI", [128, 8, 8])
        MHALF = sb("MHALF", [128, 4])
        ST = sb("ST", [128, 2, 4, 6])
        MV = sb("MV", [128, 2, 4, 2])
        VE = sb("VE", [128, 2, 4])
        RS = sb("RS", [128, 2, 4])
        XN = sb("XN", [128, 2, 4, 128])
        XT = sb("XT", [128, 2, TC])
        LG = sb("LG", [128, 2, 2, 8])
        CP = sb("CP", [128, 2, 8, 8])
        CQ = sb("CQ", [128, 2, 8, 8])
        RK = sb("RK", [128, 2, 8])
        SM = sb("SM", [128, 4, 2, 8])
        MXS = sb("MXS", [128, 8])
        GS = sb("GS", [128, 2, 2, 4])
        GA = sb("GA", [128, 8, 128])
        WB = sb("WB", [128, 2, 2, 128])

        early = ExitStack()

        def se(name, shape, dt=F32):
            return early.enter_context(nc.sbuf_tensor(name, shape, dt))

        W5 = se("W5", [128, 5632])
        WH = se("WH", [128, 5632], F32R)
        WL = se("WL", [128, 5632], F32R)

        sems = {n: sem("s_" + n) for n in ("pe", "act", "dve", "pool", "sp")}
        pe, act, dve, pool, sp = (Queue(sems[n]) for n in ("pe", "act", "dve", "pool", "sp"))
        PSA = ctx.enter_context(nc.psum_tensor("PSA", [128, 8, 512], F32))

        def bank(i):
            return PSA[:, i, :]

        def dma(q, out_ap, in_ap, s, waits=()):
            def f(e):
                e.dma_start(out_ap, in_ap).then_inc(s, 16)
            q.ops.append((f, [w for w in waits if w is not None], False, False))

        s_w = [sem(f"s_w{i}") for i in range(6)]
        s_x = [sem(f"s_x{i}") for i in range(NC)]
        xin = I["x"].rearrange("b (c p) d -> p (b c) d", p=128)
        xout = out.rearrange("b (c p) d -> p (b c) d", p=128)
        dma(sp, X[:, 0:4, :], xin[:, 0:4, :], s_x[0])
        dma(sp, IDN[:, :], I["ident"], s_w[0])
        dma(sp, W5[:, 0:1024], I["w5"][:, 0:1024], s_w[1])
        dma(sp, SC[:, :], I["sc"], s_w[0])
        dma(sp, MHALF[:, :], I["mhalf"], s_w[0])
        t_x = [Tok(s_x[c], 16) for c in range(NC)]
        t_w0 = Tok(s_w[0], 48)
        t_w1 = Tok(s_w[1], 16)
        dma(sp, W5[:, 1024:3072], I["w5"][:, 1024:3072], s_w[2])
        dma(sp, X[:, 4:8, :], xin[:, 4:8, :], s_x[1])
        dma(sp, W5[:, 3072:5632], I["w5"][:, 3072:5632], s_w[3])
        t_w2, t_w3 = Tok(s_w[2], 16), Tok(s_w[3], 16)
        for c in range(2, NC):
            dma(sp, X[:, 4 * c:4 * c + 4, :], xin[:, 4 * c:4 * c + 4, :], s_x[c])
        n4 = 0
        for dst, src in ((TH[:, :], "th"), (PG[:, :], "pg"), (WR[:, :], "wr"), (AE[:, :, :], "ae"), (BT[:, :, :], "bt"),
                         (WQ[:, :, :], "wq"), (WO[:, :], "wo"), (TRI[:, :, :], "tri"), (HIDN[:, :], "hident")):
            dma(sp, dst, I[src], s_w[4])
            n4 += 16
        t_w4 = Tok(s_w[4], n4)

        t_c = pool.put(memset(MKB[:, :], 0.0))
        t_c = pool.put(affine_select(
            out=MKB[:, :].rearrange("p (v k) -> p v k", v=4), in_=MKB[:, :].rearrange("p (v k) -> p v k", v=4),
            compare_op=ALU.is_ge, fill=NEG, base=0, pattern=[[0, 4], [-1, 128]], channel_multiplier=1), [t_c])
        t_ib = pool.put(tensor_copy(IDB[:, :], IDN[:, :]), [t_w0])

        t_wh, t_wl = {}, {}
        parts = [(0, 1024, t_w1), (1024, 3072, t_w2), (3072, 5632, t_w3)]

        def split_weights(k):
            a, b, t = parts[k]
            t_wh[k] = pool.put(tensor_copy(WH[:, a:b], W5[:, a:b]), [t])
            t_wl[k] = dve.put(tensor_tensor(WL[:, a:b], W5[:, a:b], WH[:, a:b], ALU.subtract), [t_wh[k]])

        for k in range(3):
            split_weights(k)

        t_X = list(t_x)
        lnr = Ring(2)
        xtr = Ring(2)

        def layer_norm(c):
            i, free = lnr.take()
            for j in range(4):
                t = dve.put(bn_stats(ST[:, i, j, :], X[:, 4 * c + j, :]), [t_X[c]] + free)
            for j in range(4):
                ta = dve.put(bn_aggr(MV[:, i, j, :], ST[:, i, j, :]), [t])
            tv = dve.put(tensor_scalar(VE[:, i, :], MV[:, i, :, 1], EPS, None, ALU.add), [ta])
            tr = pool.put(tensor_tensor(RS[:, i, :], VE[:, i, :], MHALF[:, :], ALU.pow), [tv, t_w0])
            for j in range(4):
                tn = dve.put(tensor_scalar(XN[:, i, j, :], X[:, 4 * c + j, :], MV[:, i, j, 0:1],
                                                            RS[:, i, j:j + 1], ALU.subtract, ALU.mult), [tr])
            return i, tn

        def transposes(i, tn, b, free):
            for j in range(4):
                t = pe.put(transpose(PSA[:, b, 128 * j:128 * j + 128], XN[:, i, j, :], IDN[:, :]),
                           [tn, t_w0] + free)
            lnr.free[i] = [t]
            return t

        pr = Ring(8)

        NT = 2
        fb = []
        for n in range(NT):
            fb.append({k: se(f"{k}{n}", [128, w * TC], F32R)
                       for k, w in (("xh", 1), ("xl", 1), ("ah", 4), ("al", 4), ("bh", 4), ("bl", 4))})
            fb[n]["y"] = se(f"y{n}", [128, TC])
        gbuf = [se(f"g{n}", [128, TC]) for n in range(2)]
        hbuf = [se(f"h{n}", [128, TC]) for n in range(3)]
        fr = Ring(NT)
        gr = Ring(2)
        hr = Ring(3)
        ffn_last = []

        def split(h, th, hi, lo, free):
            ta = pool.put(tensor_copy(hi, h), [th] + free)
            tb = dve.put(tensor_tensor(lo, h, hi, ALU.subtract), [ta])
            return tb

        def ffn(c):
            f, ffree = fr.take()
            B = fb[f]
            i, tn = layer_norm(c)
            yield
            b, free = pr.take()
            tt = transposes(i, tn, b, free)
            th = act.put(activation(B["xh"][:, :], bank(b), ACT.Copy), [tt] + ffree)
            tl = dve.put(tensor_tensor(B["xl"][:, :], bank(b), B["xh"][:, :], ALU.subtract), [th])
            pr.free[b] = [tl]
            yield

            def group(o, wcol, hi, lo, kn, waits):
                n = 2 * kn
                for k in range(kn):
                    c0, m = wcol(k), hi(k)
                    pe.put(matmul(o, WH[:, c0:c0 + 128], m, start=(k == 0), stop=False),
                           waits, inc=False)
                    pe.put(matmul(o, WL[:, c0:c0 + 128], m, start=False, stop=False),
                           [], lo=True, inc=False)
                for k in range(kn):
                    c0, m = wcol(k), lo(k)
                    if k < kn - 1:
                        pe.put(matmul(o, WH[:, c0:c0 + 128], m, start=False,
                                                              stop=False), inc=False)
                    else:
                        t = pe.put(matmul(o, WH[:, c0:c0 + 128], m, start=False,
                                                                  stop=True))
                return t

            for j in range(4):
                b1, free1 = pr.take()
                t1 = group(bank(b1), lambda k: 128 * j, lambda k: B["xh"][:, :], lambda k: B["xl"][:, :], 1,
                           [tl, t_wh[0], t_wl[0]] + free1)
                b2, free2 = pr.take()
                t2 = group(bank(b2), lambda k: 512 + 128 * j, lambda k: B["xh"][:, :], lambda k: B["xl"][:, :], 1,
                           [tl, t_wh[0]] + free2)
                g, gfree = gr.take()
                ta = act.put(activation(gbuf[g][:, :], bank(b1), ACT.Silu,
                                                                     scale=SC[:, j:j + 1]), [t1, t_w0] + gfree)
                pr.free[b1] = [ta]
                h, hfree = hr.take()
                th = dve.put(scalar_tensor_tensor(
                    out=hbuf[h][:, :], in0=bank(b2), scalar=SC[:, 4 + j:5 + j], in1=gbuf[g][:, :], op0=ALU.mult, op1=ALU.mult),
                    [t2, ta] + hfree)
                pr.free[b2] = [th]
                gr.free[g] = [th]
                ts = split(hbuf[h][:, :], th, B["ah"][:, TC * j:TC * j + TC], B["al"][:, TC * j:TC * j + TC], [])
                hr.free[h] = [ts]
            yield
            tin = ts
            for lay, (sh, sl, dh, dl) in enumerate((("ah", "al", "bh", "bl"), ("bh", "bl", "ah", "al"))):
                k0 = 1024 + 2048 * lay
                tl2 = []
                for j in range(4):
                    b1, free1 = pr.take()
                    t1 = group(bank(b1), lambda k: k0 + 512 * k + 128 * j,
                               lambda k: B[sh][:, TC * k:TC * k + TC], lambda k: B[sl][:, TC * k:TC * k + TC], 4,
                               [tin, t_wh[1 + lay], t_wl[1 + lay]] + free1)
                    tl2.append(t1)
                    h, hfree = hr.take()
                    ta = act.put(activation(
                        hbuf[h][:, :], bank(b1), ACT.Gelu, scale=SC[:, 8 + 4 * lay + j:9 + 4 * lay + j]), [t1] + hfree)
                    pr.free[b1] = [ta]
                    ts = split(hbuf[h][:, :], ta, B[dh][:, TC * j:TC * j + TC], B[dl][:, TC * j:TC * j + TC],
                               [tprev] if lay else [])
                    hr.free[h] = [ts]
                tprev = tl2[-1]
                tin = ts
                yield
            b1, free1 = pr.take()
            t1 = group(bank(b1), lambda k: 5120 + 128 * k, lambda k: B["ah"][:, TC * k:TC * k + TC],
                       lambda k: B["al"][:, TC * k:TC * k + TC], 4, [tin] + free1)
            ty = act.put(activation(B["y"][:, :], bank(b1), ACT.Copy, scale=SC[:, 16:17]), [t1])
            pr.free[b1] = [ty]
            yield
            b2, free2 = pr.take()
            for j in range(4):
                t2 = pe.put(transpose(PSA[:, b2, 128 * j:128 * j + 128],
                                                       B["y"][:, 128 * j:128 * j + 128], IDN[:, :]), [ty] + free2)
            tx = dve.put(scalar_tensor_tensor(
                out=X[:, 4 * c:4 * c + 4, :].rearrange("p a d -> p (a d)"), in0=bank(b2), scalar=0.5,
                in1=X[:, 4 * c:4 * c + 4, :].rearrange("p a d -> p (a d)"), op0=ALU.mult, op1=ALU.add), [t2])
            pr.free[b2] = [tx]
            fr.free[f] = [t1, t2, tx]
            t_X[c] = tx

        def residual(c, b, t):
            tx = dve.put(tensor_tensor(
                X[:, 4 * c:4 * c + 4, :].rearrange("p a d -> p (a d)"), bank(b),
                X[:, 4 * c:4 * c + 4, :].rearrange("p a d -> p (a d)"), ALU.add), [t])
            t_X[c] = tx
            return tx

        def normed_T(c, ring):
            i, tn = layer_norm(c)
            yield
            b, free = ring.take()
            tt = transposes(i, tn, b, free)
            x, xfree = xtr.take()
            te = act.put(activation(XT[:, x, :], bank(b), ACT.Copy), [tt] + xfree)
            ring.free[b] = [te]
            yield (i, x, te)

        THT = se("THT", [32, 2, TC])
        PH = se("PH", [128, 2, 4, 160])
        MM = se("MM", [32, 2, 2, 128])
        l0r = Ring(2)

        def attn0(c):
            q, qfree = l0r.take()
            g = normed_T(c, pr)
            next(g)
            yield
            i, x, te = next(g)
            yield
            b, free = pr.take()
            t = pe.put(matmul(PSA[0:32, b, :], TH[:, :], XT[:, x, :], start=True, stop=True),
                       [te, t_w4] + free)
            t0 = act.put(activation(THT[:, q, :], PSA[0:32, b, :], ACT.Copy), [t] + qfree)
            pr.free[b] = [t0]
            for h in range(2):
                b, free = pr.take()
                for j in range(2):
                    k = 2 * h + j
                    t = pe.put(matmul(PSA[:, b, 160 * j:160 * j + 160],
                                                                 XT[:, x, 128 * k:128 * k + 128], PG[:, :],
                                                                 start=True, stop=True), [te, t_w4] + free)
                tp = act.put(activation(
                    PH[:, q, 2 * h:2 * h + 2, :].rearrange("p a d -> p (a d)"), PSA[:, b, 0:320], ACT.Copy),
                    [t] + qfree)
                pr.free[b] = [tp]
            xtr.free[x] = [t]
            yield
            b, free = pr.take()
            for h in range(2):
                for j in range(2):
                    k = 2 * h + j
                    t = pe.put(matmul(PSA[0:32, b, 128 * h:128 * h + 128],
                                                                 PH[:, q, k, 0:32], PH[:, q, k, 32:160],
                                                                 start=(j == 0), stop=(j == 1)), [tp] + free)
            tm = act.put(activation(MM[:, q, :, :].rearrange("p a d -> p (a d)"), PSA[0:32, b, 0:256],
                                                ACT.Copy, scale=float(1.0 / np.sqrt(128.0))), [t] + qfree)
            pr.free[b] = [tm]
            yield
            b, free = pr.take()
            for k in range(4):
                t = pe.put(matmul(PSA[:, b, 128 * k:128 * k + 128],
                                                   THT[:, q, 128 * k:128 * k + 128], MM[:, q, k // 2, :],
                                                   start=True, stop=True), [tm, t0] + free)
            l0r.free[q] = [t]
            pr.free[b] = [residual(c, b, t)]

        moer = Ring(2)
        small = [None]
        gafree = [[]]

        def moe(c, ring):
            q, qfree = moer.take()
            g = normed_T(c, ring)
            next(g)
            yield
            i, x, te = next(g)
            yield
            b, free = ring.take()
            for h in range(2):
                t = pe.put(matmul(PSA[:, b, 8 * h:8 * h + 8],
                                                   XT[:, x, 256 * h:256 * h + 1].to_broadcast([128, 128]),
                                                   WR[:, :], start=True, stop=True), [te, t_w4] + free)
            L = LG[:, q, :, :]
            tl = dve.put(tensor_copy(L.rearrange("p a d -> p (a d)"), PSA[:, b, 0:16]), [t, small[0]] + qfree)
            ring.free[b] = [tl]
            for h in range(2):
                Lj = LG[:, q, h:h + 1, :].to_broadcast([128, 8, 8])
                Li = LG[:, q, h, :].rearrange("p (i o) -> p i o", o=1).to_broadcast([128, 8, 8])
                ta = dve.put(tensor_tensor(CP[:, h, :, :], Lj, Li, ALU.is_gt), [tl])
                tb = dve.put(tensor_tensor(CQ[:, h, :, :], Lj, Li, ALU.is_equal), [tl])
                tm_ = dve.put(reduce_max(MXS[:, h:h + 1], LG[:, q, h, :], AX), [tl])
                tb = dve.put(tensor_tensor(CQ[:, h, :, :], CQ[:, h, :, :], TRI[:, :, :], ALU.mult),
                             [tb])
                ta = dve.put(tensor_tensor(CP[:, h, :, :], CP[:, h, :, :], CQ[:, h, :, :], ALU.add),
                             [tb, ta])
                tr_ = dve.put(tensor_reduce(RK[:, h, :], CP[:, h, :, :], AX, ALU.add), [ta])
                ts = dve.put(tensor_scalar(SM[:, 0, h, :], LG[:, q, h, :], MXS[:, h:h + 1], None,
                                                            ALU.subtract), [tm_])
            te_ = act.put(activation(SM[:, 1, :, :], SM[:, 0, :, :], ACT.Exp), [ts])
            tk = dve.put(tensor_scalar(SM[:, 2, :, :], RK[:, :, :], 2.0, None, ALU.is_lt), [tr_])
            tk = dve.put(tensor_tensor(SM[:, 3, :, :], SM[:, 1, :, :], SM[:, 2, :, :], ALU.mult), [tk, te_])
            tz = dve.put(tensor_reduce(MXS[:, 2:4], SM[:, 3, :, :], AX, ALU.add), [tk])
            tz = dve.put(reciprocal(MXS[:, 4:6], MXS[:, 2:4]), [tz])
            for h in range(2):
                for p in range(2):
                    tg = dve.put(tensor_scalar(
                        GS[64 * p:64 * p + 64, q, h, :],
                        SM[64 * p:64 * p + 64, 3, h, :].rearrange("p (c t) -> p c t", t=2)[:, :, p],
                        MXS[64 * p:64 * p + 64, 4 + h:5 + h], None, ALU.mult), [tz])
            small[0] = tg
            yield
            for h in range(2):
                for k in range(4):
                    tga = pool.put(tensor_scalar(GA[:, 4 * h + k, :], AE[:, k, :],
                                                                      GS[:, q, h, k:k + 1], 1.0, ALU.mult, ALU.mult),
                                   [tg] + gafree[0])
            b, free = ring.take()
            for h in range(2):
                for k in range(4):
                    t = pe.put(matmul(PSA[:, b, 128 * h:128 * h + 128], GA[:, 4 * h + k, :],
                                                            BT[:, k, :], start=(k == 0), stop=(k == 3)),
                               [tga] + free)
            gafree[0] = [t]
            for h in range(2):
                tw = dve.put(scalar_tensor_tensor(
                    out=WB[:, q, h, :], in0=PSA[:, b, 128 * h:128 * h + 128], scalar=0.5, in1=HIDN[:, :],
                    op0=ALU.mult, op1=ALU.add), [t])
            ring.free[b] = [tw]
            yield
            b, free = ring.take()
            for k in range(4):
                t = pe.put(matmul(PSA[:, b, 128 * k:128 * k + 128],
                                                   XT[:, x, 128 * k:128 * k + 128], WB[:, q, k // 2, :],
                                                   start=True, stop=True), [tw] + free)
            xtr.free[x] = [t]
            moer.free[q] = [t]
            ring.free[b] = [residual(c, b, t)]

        tasks = ([ffn(c) for c in range(NC)] + [attn0(c) for c in range(NC)] + [ffn(c) for c in range(NC)]
                 + [moe(c, pr) for c in range(NC)])
        staggered(tasks, 2)

        early.close()
        dead = [t for fl in fr.free + l0r.free for t in fl] + [t_wl[2]]
        QS = [sb(f"QS{n}", [128, NH, S], F32R) for n in range(4)]
        KS = [sb(f"KS{n}", [128, 4, S], F32R) for n in range(4)]
        PB = [sb(f"PB{n}", [128, 1536]) for n in range(2)]
        RA = [sb(f"RA{n}", [128, TC]) for n in range(2)]
        CB = [sb(f"CB{n}", [128, TC], F32R) for n in range(4)]
        OT = [sb(f"OT{n}", [128, 4, TC]) for n in range(2)]
        COS = sb("COS", [128, TC])
        SIN = sb("SIN", [128, TC])
        VC = sb("VC", [128, TC])
        LC = sb("LC", [128, TC])
        RC = sb("RC", [128, TC])
        ON = sb("ON", [128, TC])
        VA = [sb(f"VA{n}", [128, 2, NH, 32]) for n in range(4)]
        MX = sb("MX", [128, 2, 2, NH])
        MT = sb("MT", [NH, 2, 2, S], F32R)
        DQ = nc.dram_tensor("dq", [NC, 4, 128, TC], F32)
        DV = nc.dram_tensor("dv", [NC, 128, TC], F32)
        DL = nc.dram_tensor("dl", [NC, NH, TC], F32)
        s_dq = [sem(f"s_dq{c}") for c in range(NC)]
        s_qs = [sem(f"s_qs{u}") for u in range(NB)]
        s_m = [sem(f"s_m{u}") for u in range(NB)]
        s_dv = [sem(f"s_dv{c}") for c in range(NC)]
        s_vl = [sem(f"s_vl{c}") for c in range(NC)]
        s_cs = sem("s_cs")
        for dst, src in ((COS, "cos"), (SIN, "sin")):
            dma(sp, dst[:, :], I[src], s_cs, dead)
        t_cs = Tok(s_cs, 32)
        SCALE = float(1.0 / np.sqrt(np.float32(DK)))

        last_moe = [t for fl in pr.free for t in fl]
        t_z = []
        for n in range(4):
            za = pool.put(memset(QS[n][:, :, :].bitcast(F32), 0.0), dead)
            zb = pool.put(memset(KS[n][96:128, :, :].bitcast(F32), 1.0), dead + [za])
            zc = pool.put(memset(VA[n][:, :, :, 8:32], 1.0), dead + [zb])
            t_z.append([za, zb, zc])
            dead = dead + [zc]

        msr = Ring(2)
        MB = [6, 7]
        msr.free = [list(last_moe), list(last_moe)]

        class Misc:
            def take(self):
                k, f = msr.take()
                return MB[k], f

            class free_(list):
                pass

        class BankFree:
            def __setitem__(self, b, toks):
                msr.free[b - 6] = toks

        misc = Misc()
        misc.free = BankFree()

        t_dq, t_qs, t_m, t_v, t_xt = {}, {}, {}, {}, {}
        cb_free = [[], []]
        ra_free = [[]]
        qfree = [[z for z in zz] + dead for zz in t_z]
        vfree = [[zz[2]] for zz in t_z]

        def prep(c):
            g = normed_T(c, misc)
            next(g)
            yield
            i, x, te = next(g)
            yield
            for side in range(2):
                ba, fa = misc.take()
                t1 = pe.put(matmul(bank(ba), WQ[:, 2 * side, :], XT[:, x, :], start=True, stop=True),
                            [te, t_w4] + fa)
                bb, fb_ = misc.take()
                t2 = pe.put(matmul(bank(bb), WQ[:, 2 * side + 1, :], XT[:, x, :], start=True, stop=True),
                            [te, t_w4] + fb_)
                ta = dve.put(tensor_tensor(RA[0][:, :], bank(ba), COS[:, :], ALU.mult),
                             [t1, t_cs] + ra_free[0] + dead)
                misc.free[ba] = [ta]
                tb = dve.put(tensor_tensor(RA[1][:, :], bank(bb), SIN[:, :], ALU.mult), [t2])
                misc.free[bb] = [tb]
                ts = pool.put(tensor_tensor(RA[0][:, :], RA[0][:, :], RA[1][:, :], ALU.add), [ta, tb])
                th = pool.put(tensor_copy(CB[2 * side][:, :], RA[0][:, :]), [ts] + cb_free[side])
                tl = dve.put(tensor_tensor(CB[2 * side + 1][:, :], RA[0][:, :], CB[2 * side][:, :],
                                                       ALU.subtract), [th])
                ra_free[0] = [tl]
                for n in (2 * side, 2 * side + 1):
                    dma(sp, DQ[c, n], CB[n][:, :].bitcast(F32), s_dq[c], [th, tl])
                cb_free[side] = [Tok(s_dq[c], 64)]
                yield
            t_dq[c] = Tok(s_dq[c], 64)
            t_xt[c] = (x, te)

        def values(c):
            x, te = t_xt[c]
            b, free = misc.take()
            for k in range(4):
                t = pe.put(matmul(PSA[:, b, 128 * k:128 * k + 128], XT[:, x, 128 * k:128 * k + 128],
                                                   WQ[:, 4, :], start=True, stop=True), [te] + free)
            xtr.free[x] = [t]
            for h in range(2):
                u = 2 * c + h
                tv = act.put(activation(
                    VA[u % 4][:, :, :, 0:8],
                    PSA[:, b, 256 * h:256 * h + 256].rearrange("p (k h d) -> p k h d", k=2, h=NH), ACT.Copy),
                    [t] + vfree[u % 4] + dead)
                t_v[u] = tv
            misc.free[b] = [tv]

        def reloc(u):
            c, h = divmod(u, 2)
            w = [t_dq[c]] + qfree[u % 4]
            K, Q = KS[u % 4], QS[u % 4]
            cols = slice(S * h, S * h + S)
            for t, n in enumerate((2, 2, 3)):
                dma(sp, K[32 * t:32 * t + 32, :, :].bitcast(F32),
                    DQ[c, n].rearrange("(g r) t -> r g t", g=4)[:, :, cols], s_qs[u], w)
            for t, n in enumerate((0, 1, 0)):
                for v in range(4):
                    dma(sp, Q[32 * t + 8 * v:32 * t + 8 * v + 8, :, :].bitcast(F32)
                        .rearrange("p (g v) t -> p g v t", v=4)[:, :, v, :],
                        DQ[c, n].rearrange("(g v d) t -> v d g t", g=4, v=4)[v][:, :, cols], s_qs[u], w)
            t_qs[u] = Tok(s_qs[u], 15 * 16)

        t_r = [None, None]
        t_mx = {}
        mxfree = [[], []]

        def pass1(u, g):
            K, Q = KS[u % 4], QS[u % 4]
            w = [t_qs[u], t_ib] + (last_moe if u == 0 and g == 0 else [])
            for v in range(4):
                pe.put(matmul(PSA[:, 2, 128 * v:128 * v + 128], Q[0:96, 4 * g + v, 0:128],
                                               K[0:96, g, 0:128], start=(v == 0), stop=False, skip_group_check=True),
                       w + [t_r[0]], inc=False)
            ta = pe.put(matmul(PSA[:, 2, :], IDB[:, :], MKB[:, :], start=False, stop=True,
                                           skip_group_check=True))
            for p in range(2):
                for v in range(2):
                    pe.put(matmul(PSA[:, p, 256 * v:256 * v + 256],
                                                        Q[0:96, 4 * g + 2 * p + v, 128:256], K[0:96, g, :],
                                                        start=(v == 0), stop=False, skip_group_check=True),
                           w + [t_r[1]], inc=False)
                tb = pe.put(matmul(
                    PSA[:, p, :].rearrange("p (v k) -> p v k", v=2)[:, :, 128:256], IDB[:, :],
                    MKB[:, 0:256].rearrange("p (v k) -> p v k", v=2), start=False, stop=True, skip_group_check=True))
            t_r[0] = dve.put(tensor_reduce(
                MX[:, u % 2, 0, 4 * g:4 * g + 4], PSA[:, 2, :].rearrange("p (v k) -> p v k", v=4), AX, ALU.max),
                [ta] + mxfree[u % 2])
            t_r[1] = dve.put(tensor_reduce(
                MX[:, u % 2, 1, 4 * g:4 * g + 4],
                PSA[:, 0:2, :].rearrange("p b (v k) -> p (b v) k", v=2), AX, ALU.max), [tb])
            if g == 3:
                b, free = misc.take()
                for k in range(2):
                    t = pe.put(transpose(PSA[0:NH, b, 128 * k:128 * k + 128], MX[:, u % 2, k, :],
                                                          IDN[:, :]), [t_r[0], t_r[1]] + free)
                mxfree[u % 2] = [t]
                th = dve.put(tensor_scalar(MT[:, u % 2, 0, :], PSA[0:NH, b, 0:256], -1.0, None, ALU.mult),
                             [t, Tok(s_m[u - 2], 32) if u >= 2 else None])
                tl = dve.put(scalar_tensor_tensor(
                    out=MT[:, u % 2, 1, :], in0=PSA[0:NH, b, 0:256], scalar=-1.0, in1=MT[:, u % 2, 0, :],
                    op0=ALU.mult, op1=ALU.subtract), [th])
                misc.free[b] = [tl]
                for k in range(2):
                    dma(sp, Q[96 + k:97 + k, :, :].bitcast(F32), MT[:, u % 2, k, :].bitcast(F32), s_m[u], [th, tl])
                t_m[u] = Tok(s_m[u], 32)

        t_e = [None]
        t_pb = {}
        pbfree = [[], []]
        nslot = [0]
        otfree = [[], []]
        t_ot = {}

        def pass2(u, g):
            K, Q = KS[u % 4], QS[u % 4]
            w = [t_m[u], t_e[0]] + (last_moe if u == 0 and g == 0 else [])
            for v in range(4):
                pe.put(matmul(PSA[:, 3 + v // 2, 256 * (v % 2):256 * (v % 2) + 256], K[:, g, 0:128],
                                               Q[:, 4 * g + v, :], start=(v % 2 == 0), stop=True,
                                               skip_group_check=True), w, inc=False)
            for v in range(4):
                t = pe.put(matmul(PSA[:, 5, 128 * v:128 * v + 128], K[:, g, 128:256],
                                                   Q[:, 4 * g + v, 128:256], start=(v == 0), stop=True,
                                                   skip_group_check=True), w)
            if g == 3:
                qfree[u % 4] = [t]
            p = (4 * u + g) % 2
            te = act.put(activation(PB[p][:, :], PSA[:, 3:6, :].rearrange("p a b -> p (a b)"), ACT.Exp,
                                                scale=SCALE), [t] + pbfree[p] + dead)
            t_e[0] = te
            pool.put(affine_select(
                out=PB[p][:, 0:1024].rearrange("p (v q) -> p v q", v=4)[:, :, 0:128],
                in_=PB[p][:, 0:1024].rearrange("p (v q) -> p v q", v=4)[:, :, 0:128],
                compare_op=ALU.is_ge, fill=0.0, base=0, pattern=[[0, 4], [1, 128]], channel_multiplier=-1), [te])
            t_pb[4 * u + g] = pool.put(affine_select(
                out=PB[p][:, 1024:1536].rearrange("p (v q) -> p v q", v=4),
                in_=PB[p][:, 1024:1536].rearrange("p (v q) -> p v q", v=4),
                compare_op=ALU.is_ge, fill=0.0, base=0, pattern=[[0, 4], [1, 128]], channel_multiplier=-1), [te])

        def weigh(u, g):
            p = (4 * u + g) % 2
            c, h = divmod(u, 2)
            b, free = misc.take()
            V = VA[u % 4]
            for v in range(4):
                pe.put(matmul(PSA[32 * v:32 * v + 32, b, 0:256], V[:, 0, 4 * g + v, :],
                                               PB[p][:, 256 * v:256 * v + 256], start=True, stop=False),
                       [t_pb[4 * u + g], t_v[u], t_v[2 * c + 1]] + free, inc=False)
            for v in range(4):
                t = pe.put(matmul(PSA[32 * v:32 * v + 32, b, 128:256], V[:, 1, 4 * g + v, :],
                                                   PB[p][:, 1024 + 128 * v:1152 + 128 * v], start=False, stop=True))
            pbfree[p] = [t]
            if g == 3:
                vfree[u % 4] = [t]
            to = act.put(activation(OT[c % 2][:, g, S * h:S * h + S], PSA[:, b, 0:256], ACT.Copy),
                         [t] + otfree[c % 2] + dead)
            misc.free[b] = [to]
            t_ot[c] = to

        vcfree = [[]]

        def fin(c):
            O = OT[c % 2]
            for v in range(4):
                dma(sp, DV[c].rearrange("(g v d) t -> v d g t", g=4, v=4)[v], O[32 * v:32 * v + 8, :, :], s_dv[c],
                    [t_ot[c]])
                dma(sp, DL[c].rearrange("(g v) t -> v g t", v=4)[v:v + 1], O[32 * v + 8:32 * v + 9, :, :], s_dv[c],
                    [t_ot[c]])
            td = Tok(s_dv[c], 128)
            otfree[c % 2] = [td]
            yield
            dma(sp, VC[:, :], DV[c], s_vl[c], [td] + vcfree[0] + dead)
            dma(sp, LC[:, :], DL[c].rearrange("h (o t) -> h o t", o=1).to_broadcast([NH, 8, TC]), s_vl[c],
                [td] + vcfree[0] + dead)
            yield
            yield
            tr = dve.put(reciprocal(RC[:, :], LC[:, :]), [Tok(s_vl[c], 32)] + dead)
            to = dve.put(tensor_tensor(ON[:, :], VC[:, :], RC[:, :], ALU.mult), [tr] + vcfree[0])
            vcfree[0] = [to]
            yield
            b, free = misc.take()
            for k in range(4):
                t = pe.put(matmul(PSA[:, b, 128 * k:128 * k + 128], ON[:, 128 * k:128 * k + 128],
                                                   WO[:, :], start=True, stop=True), [to] + free)
            vcfree[0] = [t]
            misc.free[b] = [residual(c, b, t)]

        jobs = []

        def step():
            for j in list(jobs):
                if next(j, "end") == "end":
                    jobs.remove(j)

        for s in range(-16, 4 * NB + LEAD + 2):
            for c in range(NC):
                if s == 8 * c - 12:
                    jobs.append(prep(c))
            step()
            if (s + 5) % 4 == 0 and 0 <= (s + 5) // 4 < NB:
                reloc((s + 5) // 4)
            if s % 8 == 0 and 0 <= s // 8 < NC:
                values(s // 8)
            if 0 <= s < 4 * NB:
                pass1(s // 4, s % 4)
            k = s - LEAD
            if 0 <= k < 4 * NB:
                pass2(k // 4, k % 4)
            k -= 1
            if 0 <= k < 4 * NB:
                weigh(k // 4, k % 4)
                if k % 8 == 7:
                    jobs.append(fin(k // 8))
        while jobs:
            step()

        pr.free = [[t_r[0], t_r[1]]] * 3 + [[t_e[0]]] * 3 + list(msr.free)
        pr.i = -1
        s_out = sem("s_out")

        def last(c):
            g = moe(c, pr)
            for _ in g:
                yield
            dma(sp, xout[:, 4 * c:4 * c + 4, :], X[:, 4 * c:4 * c + 4, :], s_out, [t_X[c]])

        staggered([last(c) for c in range(NC)], 2)

        def end(e):
            e.wait_ge(s_out, 16 * NC)
        sp.ops.append((end, [], False, False))

        block = ctx.enter_context(nc.Block())

        @block.sync
        def _(e):
            sp.play(e)

        @block.tensor
        def _(e):
            pe.play(e)

        @block.vector
        def _(e):
            dve.play(e)

        @block.scalar
        def _(e):
            act.play(e)

        @block.gpsimd
        def _(e):
            pool.play(e)


def kernel(**inputs):
    import concourse.bacc as bacc
    from concourse.bass_utils import run_bass_kernel_spmd

    w = {k: np.ascontiguousarray(v) for k, v in inputs.items()}
    T = lambda a: np.ascontiguousarray(a.T)

    def rows(a):
        return np.ascontiguousarray(a.reshape(-1, 128, a.shape[1]).transpose(1, 0, 2).reshape(128, -1))

    sw = np.arange(128) ^ 1
    arrays = {"x": w["L0_attn_x"]}
    arrays["w5"] = np.concatenate([T(w["L0_ffn_w1_w"]), T(w["L0_ffn_w2_w"]), rows(T(w["L0_ffn_h1_w"])),
                                   rows(T(w["L0_ffn_h2_w"])), rows(T(w["L0_ffn_w3_w"]))], axis=1)
    arrays["sc"] = np.concatenate([w[f"L0_ffn_{n}_s"].reshape(-1, 128).T for n in ("w1", "w2", "h1", "h2", "w3")],
                                  axis=1)
    arrays["th"] = T(w["L0_attn_W_theta"])
    arrays["pg"] = np.concatenate([T(w["L0_attn_W_phi"]), T(w["L0_attn_W_g"])], axis=1)
    arrays["wr"] = T(w["L1_ffn_Wr"])
    arrays["ae"] = rows(w["L1_ffn_A"].reshape(512, 128)).reshape(128, 4, 128)
    arrays["bt"] = rows(w["L1_ffn_Bw"].transpose(0, 2, 1).reshape(512, 128)).reshape(128, 4, 128)
    q, k = w["L1_attn_W_Q"], w["L1_attn_W_K"]
    arrays["wq"] = np.stack([q.T, q[sw].T, k.T, k[sw].T, w["L1_attn_W_V"].T], axis=1)
    arrays["wo"] = T(w["L1_attn_W_O"])
    f32 = np.float32
    arrays["ident"] = np.eye(128, dtype=f32)
    arrays["hident"] = np.eye(128, dtype=f32) * f32(0.5)
    arrays["mhalf"] = np.full((128, 4), -0.5, f32)
    i, j = np.arange(8)[:, None], np.arange(8)[None, :]
    arrays["tri"] = np.ascontiguousarray(np.broadcast_to((j < i).astype(f32), (128, 8, 8)))
    inv = (f32(10000.0) ** (f32(-2.0) * np.arange(4, dtype=f32) / f32(8))).astype(f32)
    ang = np.arange(S, dtype=f32)[:, None] * inv
    d = np.arange(128) % 8
    arrays["cos"] = np.tile(np.cos(ang).astype(f32)[:, d // 2].T, (1, 2))
    arrays["sin"] = np.tile((np.sin(ang).astype(f32)[:, d // 2] * np.where(d % 2, f32(1), f32(-1))).T, (1, 2))
    arrays = {k: np.ascontiguousarray(v) for k, v in arrays.items()}

    nc = bacc.Bacc("TRN2", target_bir_lowering=False, num_devices=1)
    I = {k: nc.dram_tensor(f"in_{k}", v.shape, mybir.dt.from_np(v.dtype), kind="ExternalInput").ap()
         for k, v in arrays.items()}
    out = nc.dram_tensor("out_0", (NB, S, D), F32, kind="ExternalOutput").ap()
    build(nc, I, out)
    r = run_bass_kernel_spmd(nc, [{f"in_{k}": v for k, v in arrays.items()}], core_ids=[0])
    return r.results[0]["out_0"]
```

```python
from contextlib import ExitStack

import numpy as np
import concourse.bass as bass
from concourse import mybir

F32 = mybir.dt.float32
F32R = mybir.dt.float32r
BF16 = mybir.dt.bfloat16
ALU = mybir.AluOpType
ACT = mybir.ActivationFunctionType
AX = mybir.AxisListType.X

NB = 16
S = 256
D = 128
HID = 512
NC = 8
TC = 512
NH = 16
DHEAD = 8
EPS = 1e-5
NEG = -1.0e30
LEAD = 7


def activation(*a, **k):
    return lambda e: e.activation(*a, **k)


def affine_select(*a, **k):
    return lambda e: e.affine_select(*a, **k)


def bn_aggr(*a, **k):
    return lambda e: e.bn_aggr(*a, **k)


def bn_stats(*a, **k):
    return lambda e: e.bn_stats(*a, **k)


def matmul(*a, **k):
    return lambda e: e.matmul(*a, **k)


def memset(*a, **k):
    return lambda e: e.memset(*a, **k)


def reciprocal(*a, **k):
    return lambda e: e.reciprocal(*a, **k)


def reduce_max(*a, **k):
    return lambda e: e.reduce_max(*a, **k)


def scalar_tensor_tensor(*a, **k):
    return lambda e: e.scalar_tensor_tensor(*a, **k)


def tensor_copy(*a, **k):
    return lambda e: e.tensor_copy(*a, **k)


def tensor_reduce(*a, **k):
    return lambda e: e.tensor_reduce(*a, **k)


def tensor_scalar(*a, **k):
    return lambda e: e.tensor_scalar(*a, **k)


def tensor_tensor(*a, **k):
    return lambda e: e.tensor_tensor(*a, **k)


def transpose(*a, **k):
    return lambda e: e.transpose(*a, **k)


class Tok:
    def __init__(self, sem, val):
        self.sem, self.val = sem, val


class Queue:

    def __init__(self, sem):
        self.sem, self.n, self.ops = sem, 0, []

    def put(self, fn, waits=(), lo=False, inc=True):
        tok = None
        if inc:
            self.n += 1
            tok = Tok(self.sem, self.n)
        self.ops.append((fn, [w for w in waits if w is not None], inc, lo))
        return tok

    def play(self, eng, lo=True, start=0, stop=None):
        seen = {}
        for fn, waits, inc, is_lo in self.ops[start:stop]:
            if is_lo and not lo:
                continue
            for w in waits:
                if seen.get(id(w.sem), 0) < w.val:
                    eng.wait_ge(w.sem, w.val)
                    seen[id(w.sem)] = w.val
            ins = fn(eng)
            if inc:
                ins.then_inc(self.sem, 1)


class Ring:

    def __init__(self, ids):
        self.ids, self.i = list(ids), -1
        self.free = {k: [] for k in self.ids}

    def take(self):
        self.i = (self.i + 1) % len(self.ids)
        k = self.ids[self.i]
        free, self.free[k] = self.free[k], None
        assert free is not None, "the buffer's last readers are not issued yet"
        return k, free


def build(nc, I, out):
    with ExitStack() as ctx:
        def sb(name, shape, dt=F32):
            return ctx.enter_context(nc.sbuf_tensor(name, shape, dt))

        def sem(name):
            return ctx.enter_context(nc.semaphore(name))

        X = sb("X", [128, 32, D])
        IDN = sb("IDN", [128, 128])
        HIDN = sb("HIDN", [128, 128])
        IDB = sb("IDB", [128, 128], BF16)
        MKB = sb("MKB", [128, 512], BF16)
        SC = sb("SC", [128, 17])
        TH = sb("TH", [128, 32])
        PG = sb("PG", [128, 160])
        WR = sb("WR", [128, 8])
        AE = sb("AE", [128, 4, 128])
        BT = sb("BT", [128, 4, 128])
        WQ = sb("WQ", [128, 5, 128])
        WO = sb("WO", [128, 128])
        TRI = sb("TRI", [128, 8, 8])
        MHALF = sb("MHALF", [128, 4])
        ST = sb("ST", [128, 3, 4, 6])
        MV = sb("MV", [128, 3, 4, 2])
        VE = sb("VE", [128, 3, 4])
        RS = sb("RS", [128, 3, 4])
        XN = sb("XN", [128, 3, 4, 128])
        XT = sb("XT", [128, 3, TC])
        LG = sb("LG", [128, 2, 2, 8])
        CP = sb("CP", [128, 2, 8, 8])
        CQ = sb("CQ", [128, 2, 8, 8])
        RK = sb("RK", [128, 2, 8])
        SM = sb("SM", [128, 4, 2, 8])
        MXS = sb("MXS", [128, 8])
        GS = sb("GS", [128, 2, 2, 4])
        GA = sb("GA", [128, 8, 128])
        WB = sb("WB", [128, 2, 2, 128])

        early = ExitStack()

        def se(name, shape, dt=F32):
            return early.enter_context(nc.sbuf_tensor(name, shape, dt))

        WH = se("WH", [128, 5632], F32R)
        WL = se("WL", [128, 5632], F32R)
        NT = 2
        fb = []
        for n in range(NT):
            fb.append({k: se(f"{k}{n}", [128, w * TC], F32R)
                       for k, w in (("xh", 1), ("xl", 1), ("ah", 4), ("al", 4), ("bh", 4), ("bl", 4))})
            fb[n]["y"] = se(f"y{n}", [128, TC])
        gbuf = [se(f"g{n}", [128, TC]) for n in range(3)]
        hbuf = [se(f"h{n}", [128, TC]) for n in range(3)]
        stage = ExitStack()
        W5 = stage.enter_context(nc.sbuf_tensor("W5", [128, 5632], F32))

        sems = {n: sem("s_" + n) for n in ("pe", "act", "dve", "pool", "sp")}
        pe, act, dve, pool, sp = (Queue(sems[n]) for n in ("pe", "act", "dve", "pool", "sp"))
        PSA = ctx.enter_context(nc.psum_tensor("PSA", [128, 8, 512], F32))

        def bank(i):
            return PSA[:, i, :]

        def dma(q, out_ap, in_ap, s, waits=()):
            def f(e):
                e.dma_start(out_ap, in_ap).then_inc(s, 16)
            q.ops.append((f, [w for w in waits if w is not None], False, False))

        s_w = [sem(f"s_w{i}") for i in range(6)]
        s_x = [sem(f"s_x{i}") for i in range(NC)]
        xin = I["x"].rearrange("b (c p) d -> p (b c) d", p=128)
        xout = out.rearrange("b (c p) d -> p (b c) d", p=128)
        dma(sp, X[:, 0:4, :], xin[:, 0:4, :], s_x[0])
        dma(sp, IDN[:, :], I["ident"], s_w[0])
        dma(sp, W5[:, 0:1024], I["w5"][:, 0:1024], s_w[1])
        dma(sp, SC[:, :], I["sc"], s_w[0])
        dma(sp, MHALF[:, :], I["mhalf"], s_w[0])
        t_x = [Tok(s_x[c], 16) for c in range(NC)]
        t_w0 = Tok(s_w[0], 48)
        t_w1 = Tok(s_w[1], 16)
        dma(sp, W5[:, 1024:3072], I["w5"][:, 1024:3072], s_w[2])
        dma(sp, X[:, 4:8, :], xin[:, 4:8, :], s_x[1])
        dma(sp, W5[:, 3072:5632], I["w5"][:, 3072:5632], s_w[3])
        t_w2, t_w3 = Tok(s_w[2], 16), Tok(s_w[3], 16)
        for c in range(2, NC):
            dma(sp, X[:, 4 * c:4 * c + 4, :], xin[:, 4 * c:4 * c + 4, :], s_x[c])
        n4 = 0
        for dst, src in ((TH[:, :], "th"), (PG[:, :], "pg"), (WR[:, :], "wr"), (AE[:, :, :], "ae"), (BT[:, :, :], "bt"),
                         (WQ[:, :, :], "wq"), (WO[:, :], "wo"), (TRI[:, :, :], "tri"), (HIDN[:, :], "hident")):
            dma(sp, dst, I[src], s_w[4])
            n4 += 16
        t_w4 = Tok(s_w[4], n4)

        t_c = pool.put(memset(MKB[:, :], 0.0))
        t_c = pool.put(affine_select(
            out=MKB[:, :].rearrange("p (v k) -> p v k", v=4), in_=MKB[:, :].rearrange("p (v k) -> p v k", v=4),
            compare_op=ALU.is_ge, fill=NEG, base=0, pattern=[[0, 4], [-1, 128]], channel_multiplier=1), [t_c])
        t_ib = pool.put(tensor_copy(IDB[:, :], IDN[:, :]), [t_w0])

        t_wh, t_wl = {}, {}
        parts = [(0, 1024, t_w1), (1024, 3072, t_w2), (3072, 5632, t_w3)]

        for k, (a, b, t) in enumerate(parts):
            t_wh[k] = dve.put(tensor_copy(WH[:, a:b], W5[:, a:b]), [t])
            t_wl[k] = dve.put(tensor_tensor(WL[:, a:b], W5[:, a:b], WH[:, a:b], ALU.subtract), [t_wh[k]])

        t_X = list(t_x)
        lnr = Ring(range(3))
        xtr = Ring(range(3))

        def layer_norm(c):
            i, free = lnr.take()
            for j in range(4):
                t = dve.put(bn_stats(ST[:, i, j, :], X[:, 4 * c + j, :]), [t_X[c]] + free)
            for j in range(4):
                ta = dve.put(bn_aggr(MV[:, i, j, :], ST[:, i, j, :]), [t])
            tv = dve.put(tensor_scalar(VE[:, i, :], MV[:, i, :, 1], EPS, None, ALU.add), [ta])
            tr = pool.put(tensor_tensor(RS[:, i, :], VE[:, i, :], MHALF[:, :], ALU.pow), [tv, t_w0])
            for j in range(4):
                tn = dve.put(tensor_scalar(XN[:, i, j, :], X[:, 4 * c + j, :], MV[:, i, j, 0:1],
                                                            RS[:, i, j:j + 1], ALU.subtract, ALU.mult), [tr])
            return i, tn

        def transposes(i, tn, b, free):
            for j in range(4):
                t = pe.put(transpose(PSA[:, b, 128 * j:128 * j + 128], XN[:, i, j, :], IDN[:, :]),
                           [tn, t_w0] + free)
            lnr.free[i] = [t]
            return t

        pr = Ring(range(6))
        sr = Ring((6, 7))

        gr = Ring(range(3))
        hr = Ring(range(3))
        last_ffn = {}
        SPL = [[(dve, dve), (dve, dve), (dve, dve), (dve, dve)],
               [(dve, dve), (act, dve), (dve, dve), (act, dve)],
               [(dve, dve), (act, dve), (dve, dve), (act, dve)]]

        def split(h, th, hi, lo, q_hi, q_lo, free):
            if q_hi is act:
                ta = act.put(activation(hi, h, ACT.Copy), [th] + free)
            else:
                ta = dve.put(tensor_copy(hi, h), [th] + free)
            tb = q_lo.put(tensor_tensor(lo, h, hi, ALU.subtract), [ta])
            return ta, tb

        def group(o, cols, hi, lo, w_hi, w_lo, ready, free):
            n = len(cols)
            for k in range(n):
                w = WH[:, cols[k]:cols[k] + 128]
                wl = WL[:, cols[k]:cols[k] + 128]
                pe.put(matmul(o, w, hi[k], start=(k == 0), stop=False), [w_hi] + ready[k] + free, inc=False)
                pe.put(matmul(o, wl, hi[k], start=False, stop=False), [w_lo], lo=True, inc=False)
                t = pe.put(matmul(o, w, lo[k], start=False, stop=(k == n - 1)), inc=(k == n - 1))
            return t

        def ffn(c, after=None):
            B = fb[c % NT]
            i, tn = layer_norm(c)
            yield
            b, free = pr.take()
            tt = transposes(i, tn, b, free)
            th = act.put(activation(B["xh"][:, :], bank(b), ACT.Copy), [tt])
            tl = dve.put(tensor_tensor(B["xl"][:, :], bank(b), B["xh"][:, :], ALU.subtract), [th])
            pr.free[b] = [tl]
            yield

            def cut(name, k):
                return B[name][:, TC * k:TC * k + TC]

            ready = []
            for j in range(4):
                b1, free1 = pr.take()
                t1 = group(bank(b1), [128 * j], [B["xh"][:, :]], [B["xl"][:, :]], t_wh[0], t_wl[0], [[th, tl]], free1)
                b2, free2 = pr.take()
                t2 = group(bank(b2), [512 + 128 * j], [B["xh"][:, :]], [B["xl"][:, :]], t_wh[0], t_wl[0], [[th, tl]],
                           free2)
                g, gfree = gr.take()
                ta = act.put(activation(gbuf[g][:, :], bank(b1), ACT.Silu, scale=SC[:, j:j + 1]), [t1, t_w0] + gfree)
                pr.free[b1] = [ta]
                h, hfree = hr.take()
                th_ = dve.put(scalar_tensor_tensor(out=hbuf[h][:, :], in0=bank(b2), scalar=SC[:, 4 + j:5 + j],
                                                   in1=gbuf[g][:, :], op0=ALU.mult, op1=ALU.mult),
                              [t2, ta, t_w0] + hfree)
                pr.free[b2] = [th_]
                gr.free[g] = [th_]
                ready.append(list(split(hbuf[h][:, :], th_, cut("ah", j), cut("al", j), *SPL[0][j], [])))
                hr.free[h] = ready[-1]
            yield
            for lay, (src, dst) in enumerate((("a", "b"), ("b", "a"))):
                k0 = 1024 + 2048 * lay
                nxt, done = [], []
                for j in range(4):
                    b1, free1 = pr.take()
                    t1 = group(bank(b1), [k0 + 512 * k + 128 * j for k in range(4)],
                               [cut(src + "h", k) for k in range(4)], [cut(src + "l", k) for k in range(4)],
                               t_wh[1 + lay], t_wl[1 + lay], ready, free1)
                    done.append(t1)
                    h, hfree = hr.take()
                    ta = act.put(activation(hbuf[h][:, :], bank(b1), ACT.Gelu,
                                            scale=SC[:, 8 + 4 * lay + j:9 + 4 * lay + j]), [t1, t_w0] + hfree)
                    pr.free[b1] = [ta]
                    nxt.append(list(split(hbuf[h][:, :], ta, cut(dst + "h", j), cut(dst + "l", j), *SPL[1 + lay][j],
                                          [])))
                    hr.free[h] = nxt[-1]
                ready = nxt
                yield
            b1, free1 = pr.take()
            t1 = group(bank(b1), [5120 + 128 * k for k in range(4)], [cut("ah", k) for k in range(4)],
                       [cut("al", k) for k in range(4)], t_wh[2], t_wl[2], ready, free1)
            ty = act.put(activation(B["y"][:, :], bank(b1), ACT.Copy, scale=SC[:, 16:17]), [t1, t_w0])
            pr.free[b1] = [ty]
            yield
            b2, free2 = pr.take()
            for j in range(4):
                t2 = pe.put(transpose(PSA[:, b2, 128 * j:128 * j + 128], B["y"][:, 128 * j:128 * j + 128],
                                      IDN[:, :]), [ty] + free2)
            tx = dve.put(scalar_tensor_tensor(
                out=X[:, 4 * c:4 * c + 4, :].rearrange("p a d -> p (a d)"), in0=bank(b2), scalar=0.5,
                in1=X[:, 4 * c:4 * c + 4, :].rearrange("p a d -> p (a d)"), op0=ALU.mult, op1=ALU.add), [t2])
            pr.free[b2] = [tx]
            t_X[c] = tx
            last_ffn[c] = [t1, t2, tx]
            if after is not None:
                second.append(after)

        def residual(c, b, t):
            tx = dve.put(tensor_tensor(
                X[:, 4 * c:4 * c + 4, :].rearrange("p a d -> p (a d)"), bank(b),
                X[:, 4 * c:4 * c + 4, :].rearrange("p a d -> p (a d)"), ALU.add), [t])
            t_X[c] = tx
            return tx

        def normed_T(c, ring):
            i, tn = layer_norm(c)
            yield
            b, free = ring.take()
            tt = transposes(i, tn, b, free)
            x, xfree = xtr.take()
            te = act.put(activation(XT[:, x, :], bank(b), ACT.Copy), [tt] + xfree)
            ring.free[b] = [te]
            yield (i, x, te)

        stage.close()
        THT = se("THT", [32, 2, TC])
        PH = se("PH", [128, 2, 4, 160])
        MM = se("MM", [32, 2, 2, 128])
        l0r = Ring(range(2))

        def attn0(c):
            g = normed_T(c, sr)
            next(g)
            yield
            i, x, te = next(g)
            yield
            q, qfree = l0r.take()
            b, free = sr.take()
            t = pe.put(matmul(PSA[0:32, b, :], TH[:, :], XT[:, x, :], start=True, stop=True),
                       [te, t_w4] + free)
            t0 = act.put(activation(THT[:, q, :], PSA[0:32, b, :], ACT.Copy), [t, t_wl[2]] + qfree)
            sr.free[b] = [t0]
            for h in range(2):
                b, free = sr.take()
                for j in range(2):
                    k = 2 * h + j
                    t = pe.put(matmul(PSA[:, b, 160 * j:160 * j + 160],
                                                                 XT[:, x, 128 * k:128 * k + 128], PG[:, :],
                                                                 start=True, stop=True), [te, t_w4] + free)
                tp = act.put(activation(
                    PH[:, q, 2 * h:2 * h + 2, :].rearrange("p a d -> p (a d)"), PSA[:, b, 0:320], ACT.Copy),
                    [t] + qfree)
                sr.free[b] = [tp]
            xtr.free[x] = [t]
            yield
            b, free = sr.take()
            for h in range(2):
                for j in range(2):
                    k = 2 * h + j
                    t = pe.put(matmul(PSA[0:32, b, 128 * h:128 * h + 128],
                                                                 PH[:, q, k, 0:32], PH[:, q, k, 32:160],
                                                                 start=(j == 0), stop=(j == 1)), [tp] + free)
            tm = act.put(activation(MM[:, q, :, :].rearrange("p a d -> p (a d)"), PSA[0:32, b, 0:256],
                                                ACT.Copy, scale=float(1.0 / np.sqrt(128.0))), [t] + qfree)
            sr.free[b] = [tm]
            yield
            b, free = sr.take()
            for k in range(4):
                t = pe.put(matmul(PSA[:, b, 128 * k:128 * k + 128],
                                                   THT[:, q, 128 * k:128 * k + 128], MM[:, q, k // 2, :],
                                                   start=True, stop=True), [tm, t0] + free)
            l0r.free[q] = [t]
            sr.free[b] = [residual(c, b, t)]

        moer = Ring(range(2))
        small = [None]
        gafree = [[]]

        def moe(c, ring):
            g = normed_T(c, ring)
            next(g)
            yield
            i, x, te = next(g)
            yield
            q, qfree = moer.take()
            b, free = ring.take()
            for h in range(2):
                t = pe.put(matmul(PSA[:, b, 8 * h:8 * h + 8],
                                                   XT[:, x, 256 * h:256 * h + 1].to_broadcast([128, 128]),
                                                   WR[:, :], start=True, stop=True), [te, t_w4] + free)
            L = LG[:, q, :, :]
            tl = dve.put(tensor_copy(L.rearrange("p a d -> p (a d)"), PSA[:, b, 0:16]), [t, small[0]] + qfree)
            ring.free[b] = [tl]
            for h in range(2):
                Lj = LG[:, q, h:h + 1, :].to_broadcast([128, 8, 8])
                Li = LG[:, q, h, :].rearrange("p (i o) -> p i o", o=1).to_broadcast([128, 8, 8])
                ta = dve.put(tensor_tensor(CP[:, h, :, :], Lj, Li, ALU.is_gt), [tl])
                tb = dve.put(tensor_tensor(CQ[:, h, :, :], Lj, Li, ALU.is_equal), [tl])
                tm_ = dve.put(reduce_max(MXS[:, h:h + 1], LG[:, q, h, :], AX), [tl])
                tb = dve.put(tensor_tensor(CQ[:, h, :, :], CQ[:, h, :, :], TRI[:, :, :], ALU.mult),
                             [tb])
                ta = dve.put(tensor_tensor(CP[:, h, :, :], CP[:, h, :, :], CQ[:, h, :, :], ALU.add),
                             [tb, ta])
                tr_ = dve.put(tensor_reduce(RK[:, h, :], CP[:, h, :, :], AX, ALU.add), [ta])
                ts = dve.put(tensor_scalar(SM[:, 0, h, :], LG[:, q, h, :], MXS[:, h:h + 1], None,
                                                            ALU.subtract), [tm_])
            te_ = act.put(activation(SM[:, 1, :, :], SM[:, 0, :, :], ACT.Exp), [ts])
            tk = dve.put(tensor_scalar(SM[:, 2, :, :], RK[:, :, :], 2.0, None, ALU.is_lt), [tr_])
            tk = dve.put(tensor_tensor(SM[:, 3, :, :], SM[:, 1, :, :], SM[:, 2, :, :], ALU.mult), [tk, te_])
            tz = dve.put(tensor_reduce(MXS[:, 2:4], SM[:, 3, :, :], AX, ALU.add), [tk])
            tz = dve.put(reciprocal(MXS[:, 4:6], MXS[:, 2:4]), [tz])
            for h in range(2):
                for p in range(2):
                    tg = dve.put(tensor_scalar(
                        GS[64 * p:64 * p + 64, q, h, :],
                        SM[64 * p:64 * p + 64, 3, h, :].rearrange("p (c t) -> p c t", t=2)[:, :, p],
                        MXS[64 * p:64 * p + 64, 4 + h:5 + h], None, ALU.mult), [tz])
            small[0] = tg
            yield
            for h in range(2):
                for k in range(4):
                    tga = pool.put(tensor_scalar(GA[:, 4 * h + k, :], AE[:, k, :],
                                                                      GS[:, q, h, k:k + 1], 1.0, ALU.mult, ALU.mult),
                                   [tg] + gafree[0])
            b, free = ring.take()
            for h in range(2):
                for k in range(4):
                    t = pe.put(matmul(PSA[:, b, 128 * h:128 * h + 128], GA[:, 4 * h + k, :],
                                                            BT[:, k, :], start=(k == 0), stop=(k == 3)),
                               [tga] + free)
            gafree[0] = [t]
            for h in range(2):
                tw = dve.put(scalar_tensor_tensor(
                    out=WB[:, q, h, :], in0=PSA[:, b, 128 * h:128 * h + 128], scalar=0.5, in1=HIDN[:, :],
                    op0=ALU.mult, op1=ALU.add), [t])
            ring.free[b] = [tw]
            yield
            b, free = ring.take()
            for k in range(4):
                t = pe.put(matmul(PSA[:, b, 128 * k:128 * k + 128],
                                                   XT[:, x, 128 * k:128 * k + 128], WB[:, q, k // 2, :],
                                                   start=True, stop=True), [tw] + free)
            xtr.free[x] = [t]
            moer.free[q] = [t]
            ring.free[b] = [residual(c, b, t)]

        second = []

        def main():
            live = []
            tasks = [ffn(c, attn0(c)) for c in range(NC)] + [ffn(c, moe(c, sr)) for c in range(NC)]
            tick, n = 0, 0
            while n < len(tasks) or live or second:
                if tick % 2 == 0 and n < len(tasks):
                    live.insert(0, tasks[n])
                    n += 1
                for t in list(live):
                    if next(t, "end") == "end":
                        live.remove(t)
                for t in list(second):
                    if next(t, "end") == "end":
                        second.remove(t)
                tick += 1

        main()

        early.close()
        dead = [t for c in (NC - 2, NC - 1) for t in last_ffn[c]] + list(l0r.free[0]) + list(l0r.free[1]) + [t_wl[2]]
        QS = [sb(f"QS{n}", [128, 4, 4, S], F32R) for n in range(4)]
        KS = [sb(f"KS{n}", [128, 4, S], F32R) for n in range(4)]
        PB = [sb(f"PB{n}", [128, 1536]) for n in range(2)]
        RA = [sb(f"RA{n}", [128, TC]) for n in range(2)]
        CB = [sb(f"CB{n}", [128, TC], F32R) for n in range(4)]
        OT = [sb(f"OT{n}", [128, 4, TC]) for n in range(2)]
        COS = sb("COS", [128, TC])
        SIN = sb("SIN", [128, TC])
        VC = sb("VC", [128, TC])
        LC = sb("LC", [128, TC])
        RC = sb("RC", [128, TC])
        ON = sb("ON", [128, TC])
        VA = [sb(f"VA{n}", [128, 2, NH, 32]) for n in range(4)]
        MX = sb("MX", [128, 2, 2, 4, 4])
        MT = sb("MT", [NH, 2, 2, S], F32R)
        XP = sb("XP", [128, 2, TC])
        DQ = nc.dram_tensor("dq", [NB, 4, 3, 8, 4, S], F32)
        DKK = nc.dram_tensor("dk", [NB, 4, 3, 8, 4, S], F32)
        DO = nc.dram_tensor("do", [NC, 4, 32, 4, TC], F32)
        s_dq = [sem(f"s_dq{c}") for c in range(NC)]
        s_qs = [sem(f"s_qs{u}") for u in range(NB)]
        s_m = [sem(f"s_m{u}") for u in range(NB)]
        s_dv = [sem(f"s_dv{c}") for c in range(NC)]
        s_vl = [sem(f"s_vl{c}") for c in range(NC)]
        s_cs = sem("s_cs")
        for dst, src in ((COS, "cos"), (SIN, "sin")):
            dma(sp, dst[:, :], I[src], s_cs, dead)
        t_cs = Tok(s_cs, 32)
        SCALE = float(1.0 / np.sqrt(np.float32(DHEAD)))

        last_moe = [t for fl in pr.free.values() for t in fl]
        t_z = []
        for n in range(4):
            za = pool.put(memset(QS[n][:, :, :, :].bitcast(F32), 0.0), dead)
            zb = pool.put(memset(KS[n][96:128, :, :].bitcast(F32), 1.0), dead + [za])
            zc = pool.put(memset(VA[n][:, :, :, 8:32], 1.0), dead + [zb])
            t_z.append([za, zb, zc])
            dead = dead + [zc]

        misc = sr
        xpr = Ring(range(2))

        t_dq, t_qs, t_m, t_v, t_xt = {}, {}, {}, {}, {}
        cb_free = [[], []]
        ra_free = [[]]
        qfree = [[z for z in zz] + dead for zz in t_z]
        vfree = [[zz[2]] for zz in t_z]

        def prep(c):
            i, tn = layer_norm(c)
            yield
            b, free = misc.take()
            tt = transposes(i, tn, b, free)
            x, xfree = xpr.take()
            te = act.put(activation(XP[:, x, :], bank(b), ACT.Copy), [tt] + xfree + dead)
            misc.free[b] = [te]
            yield
            for side, dst, terms in ((1, DKK, (0, 0, 1)), (0, DQ, (0, 1, 0))):
                ba, fa = misc.take()
                t1 = pe.put(matmul(bank(ba), WQ[:, 2 * side, :], XP[:, x, :], start=True, stop=True),
                            [te, t_w4] + fa)
                bb, fb_ = misc.take()
                t2 = pe.put(matmul(bank(bb), WQ[:, 2 * side + 1, :], XP[:, x, :], start=True, stop=True),
                            [te, t_w4] + fb_)
                ta = dve.put(tensor_tensor(RA[0][:, :], bank(ba), COS[:, :], ALU.mult),
                             [t1, t_cs] + ra_free[0] + dead)
                misc.free[ba] = [ta]
                tb = dve.put(tensor_tensor(RA[1][:, :], bank(bb), SIN[:, :], ALU.mult), [t2])
                misc.free[bb] = [tb]
                ts = pool.put(tensor_tensor(RA[0][:, :], RA[0][:, :], RA[1][:, :], ALU.add), [ta, tb])
                yield
                th = dve.put(tensor_copy(CB[2 * side][:, :], RA[0][:, :]), [ts] + cb_free[side])
                tl = pool.put(tensor_tensor(CB[2 * side + 1][:, :], RA[0][:, :], CB[2 * side][:, :],
                                            ALU.subtract), [th])
                ra_free[0] = [tl]
                for t, n in enumerate(terms):
                    for u in range(2):
                        dma(sp, dst[2 * c + u, :, t].rearrange("v w g k -> v (w g) k"),
                            CB[2 * side + n][:, S * u:S * u + S].bitcast(F32), s_dq[c], [th, tl])
                cb_free[side] = [Tok(s_dq[c], 192)]
                yield
            t_dq[c] = Tok(s_dq[c], 192)
            t_xt[c] = (x, te)

        def values(c):
            x, te = t_xt[c]
            b, free = misc.take()
            for k in range(4):
                t = pe.put(matmul(PSA[:, b, 128 * k:128 * k + 128], XP[:, x, 128 * k:128 * k + 128],
                                  WQ[:, 4, :], start=True, stop=True), [te] + free)
            xpr.free[x] = [t]
            for h in range(2):
                u = 2 * c + h
                tv = act.put(activation(
                    VA[u % 4][:, :, :, 0:8],
                    PSA[:, b, 256 * h:256 * h + 256].rearrange("p (k h d) -> p k h d", k=2, h=NH), ACT.Copy),
                    [t] + vfree[u % 4] + dead)
                t_v[u] = tv
            misc.free[b] = [tv]

        def reloc(u):
            w = [t_dq[u // 2]] + qfree[u % 4]
            qfree[u % 4] = None
            K, Q = KS[u % 4], QS[u % 4]
            dma(sp, K[0:96, :, :].bitcast(F32).rearrange("p g k -> p (g k)"),
                DKK[u].rearrange("v t w g k -> (v t w) (g k)"), s_qs[u], w)
            for v in range(4):
                dma(sp, Q[24 * v:24 * v + 24, v, :, :].bitcast(F32).rearrange("p g k -> p (g k)"),
                    DQ[u, v].rearrange("t w g k -> (t w) (g k)"), s_qs[u], w)
            t_qs[u] = Tok(s_qs[u], 5 * 16)

        t_r = [None, None]
        t_mx = {}
        mxfree = [[], []]

        def pass1(u, g):
            K, Q = KS[u % 4], QS[u % 4]
            w = [t_qs[u], t_ib] + (last_moe if u == 0 and g == 0 else [])
            for v in range(4):
                pe.put(matmul(PSA[:, 2, 128 * v:128 * v + 128], Q[0:96, v, g, 0:128],
                                               K[0:96, g, 0:128], start=(v == 0), stop=False, skip_group_check=True),
                       w + [t_r[0]], inc=False)
            ta = pe.put(matmul(PSA[:, 2, :], IDB[:, :], MKB[:, :], start=False, stop=True,
                                           skip_group_check=True))
            for p in range(2):
                for v in range(2):
                    pe.put(matmul(PSA[:, p, 256 * v:256 * v + 256],
                                                        Q[0:96, 2 * p + v, g, 128:256], K[0:96, g, :],
                                                        start=(v == 0), stop=False, skip_group_check=True),
                           w + [t_r[1]], inc=False)
                tb = pe.put(matmul(
                    PSA[:, p, :].rearrange("p (v k) -> p v k", v=2)[:, :, 128:256], IDB[:, :],
                    MKB[:, 0:256].rearrange("p (v k) -> p v k", v=2), start=False, stop=True, skip_group_check=True))
            t_r[0] = dve.put(tensor_reduce(
                MX[:, u % 2, 0, :, g], PSA[:, 2, :].rearrange("p (v k) -> p v k", v=4), AX, ALU.max),
                [ta] + mxfree[u % 2])
            t_r[1] = dve.put(tensor_reduce(
                MX[:, u % 2, 1, :, g],
                PSA[:, 0:2, :].rearrange("p b (v k) -> p (b v) k", v=2), AX, ALU.max), [tb])
            if g == 3:
                b, free = misc.take()
                for k in range(2):
                    t = pe.put(transpose(PSA[0:NH, b, 128 * k:128 * k + 128],
                                          MX[:, u % 2, k, :, :].rearrange("p v g -> p (v g)"),
                                                          IDN[:, :]), [t_r[0], t_r[1]] + free)
                mxfree[u % 2] = [t]
                th = dve.put(tensor_scalar(MT[:, u % 2, 0, :], PSA[0:NH, b, 0:256], -1.0, None, ALU.mult),
                             [t, Tok(s_m[u - 2], 32) if u >= 2 else None])
                tl = dve.put(scalar_tensor_tensor(
                    out=MT[:, u % 2, 1, :], in0=PSA[0:NH, b, 0:256], scalar=-1.0, in1=MT[:, u % 2, 0, :],
                    op0=ALU.mult, op1=ALU.subtract), [th])
                misc.free[b] = [tl]
                for k in range(2):
                    dma(sp, Q[96 + k:97 + k, :, :, :].bitcast(F32).rearrange("o v g k -> o (v g) k"),
                        MT[:, u % 2, k, :].bitcast(F32), s_m[u], [th, tl])
                t_m[u] = Tok(s_m[u], 32)

        t_e = [None]
        t_pb = {}
        pbfree = [[], []]
        nslot = [0]
        otfree = [[], []]
        t_ot = {}

        def pass2(u, g):
            K, Q = KS[u % 4], QS[u % 4]
            w = [t_m[u], t_e[0]] + (last_moe if u == 0 and g == 0 else [])
            for v in range(4):
                pe.put(matmul(PSA[:, 3 + v // 2, 256 * (v % 2):256 * (v % 2) + 256], K[:, g, 0:128],
                                               Q[:, v, g, :], start=(v % 2 == 0), stop=True,
                                               skip_group_check=True), w, inc=False)
            t = pe.put(matmul(PSA[:, 5, :], K[:, g, 128:256], Q[:, :, g, 128:256], start=True, stop=True), w)
            if g == 3:
                qfree[u % 4] = [t]
            p = (4 * u + g) % 2
            te = act.put(activation(PB[p][:, :], PSA[:, 3:6, :].rearrange("p a b -> p (a b)"), ACT.Exp,
                                                scale=SCALE), [t] + pbfree[p] + dead)
            t_e[0] = te
            pool.put(affine_select(
                out=PB[p][:, 0:1024].rearrange("p (v q) -> p v q", v=4)[:, :, 0:128],
                in_=PB[p][:, 0:1024].rearrange("p (v q) -> p v q", v=4)[:, :, 0:128],
                compare_op=ALU.is_ge, fill=0.0, base=0, pattern=[[0, 4], [1, 128]], channel_multiplier=-1), [te])
            t_pb[4 * u + g] = pool.put(affine_select(
                out=PB[p][:, 1024:1536].rearrange("p (v q) -> p v q", v=4),
                in_=PB[p][:, 1024:1536].rearrange("p (v q) -> p v q", v=4),
                compare_op=ALU.is_ge, fill=0.0, base=0, pattern=[[0, 4], [1, 128]], channel_multiplier=-1), [te])

        def weigh(u, g):
            p = (4 * u + g) % 2
            c, h = divmod(u, 2)
            b, free = misc.take()
            V = VA[u % 4]
            for v in range(4):
                pe.put(matmul(PSA[32 * v:32 * v + 32, b, 0:256], V[:, 0, 4 * g + v, :],
                                               PB[p][:, 256 * v:256 * v + 256], start=True, stop=False),
                       [t_pb[4 * u + g], t_v[u], t_v[2 * c + 1]] + free, inc=False)
            for v in range(4):
                t = pe.put(matmul(PSA[32 * v:32 * v + 32, b, 128:256], V[:, 1, 4 * g + v, :],
                                                   PB[p][:, 1024 + 128 * v:1152 + 128 * v], start=False, stop=True))
            pbfree[p] = [t]
            if g == 3:
                vfree[u % 4] = [t]
            to = act.put(activation(OT[c % 2][:, g, S * h:S * h + S], PSA[:, b, 0:256], ACT.Copy),
                         [t] + otfree[c % 2] + dead)
            misc.free[b] = [to]
            t_ot[c] = to

        vcfree = [[]]

        def fin(c):
            dma(sp, DO[c].rearrange("v r g t -> (v r) (g t)"),
                OT[c % 2][:, :, :].rearrange("p g t -> p (g t)"), s_dv[c], [t_ot[c]])
            td = Tok(s_dv[c], 16)
            otfree[c % 2] = [td]
            yield
            yield
            for T, r in ((VC, 0), (LC, 8)):
                dma(sp, T[:, :],
                    DO[c, :, r:r + 8].rearrange("v r g t -> v (r g) t"), s_vl[c], [td] + vcfree[0] + dead)
            yield
            yield
            yield
            tr = dve.put(reciprocal(RC[:, :], LC[:, :]), [Tok(s_vl[c], 32)] + dead)
            to = dve.put(tensor_tensor(ON[:, :], VC[:, :], RC[:, :], ALU.mult), [tr] + vcfree[0])
            vcfree[0] = [to]
            yield
            b, free = misc.take()
            for k in range(4):
                t = pe.put(matmul(PSA[:, b, 128 * k:128 * k + 128], ON[:, 128 * k:128 * k + 128],
                                                   WO[:, :], start=True, stop=True), [to] + free)
            vcfree[0] = [t]
            misc.free[b] = [residual(c, b, t)]
            yield
            for _ in moe(c, sr):
                yield
            dma(sp, xout[:, 4 * c:4 * c + 4, :], X[:, 4 * c:4 * c + 4, :], s_out, [t_X[c]])

        s_out = sem("s_out")
        jobs = []

        def step():
            for j in list(jobs):
                if next(j, "end") == "end":
                    jobs.remove(j)

        for s in range(-16, 4 * NB + LEAD + 2):
            for c in range(NC):
                if s == 8 * c - 12:
                    jobs.append(prep(c))
            step()
            if (s + 5) % 4 == 0 and 0 <= (s + 5) // 4 < NB:
                reloc((s + 5) // 4)
            if s % 8 == 0 and 0 <= s // 8 < NC:
                values(s // 8)
            if 0 <= s < 4 * NB:
                pass1(s // 4, s % 4)
            k = s - LEAD
            if 0 <= k < 4 * NB:
                pass2(k // 4, k % 4)
            k -= 1
            if 0 <= k < 4 * NB:
                weigh(k // 4, k % 4)
                if k % 8 == 7:
                    jobs.append(fin(k // 8))
        while jobs:
            step()

        def end(e):
            e.wait_ge(s_out, 16 * NC)
        sp.ops.append((end, [], False, False))


        block = ctx.enter_context(nc.Block())

        @block.sync
        def _(e):
            sp.play(e)

        @block.tensor
        def _(e):
            pe.play(e)

        @block.vector
        def _(e):
            dve.play(e)

        @block.scalar
        def _(e):
            act.play(e)

        @block.gpsimd
        def _(e):
            pool.play(e)


def kernel(**inputs):
    import concourse.bacc as bacc
    from concourse.bass_utils import run_bass_kernel_spmd

    w = {k: np.ascontiguousarray(v) for k, v in inputs.items()}
    T = lambda a: np.ascontiguousarray(a.T)

    def rows(a):
        return np.ascontiguousarray(a.reshape(-1, 128, a.shape[1]).transpose(1, 0, 2).reshape(128, -1))

    arrays = {"x": w["L0_attn_x"]}
    arrays["w5"] = np.concatenate([T(w["L0_ffn_w1_w"]), T(w["L0_ffn_w2_w"]), rows(T(w["L0_ffn_h1_w"])),
                                   rows(T(w["L0_ffn_h2_w"])), rows(T(w["L0_ffn_w3_w"]))], axis=1)
    arrays["sc"] = np.concatenate([w[f"L0_ffn_{n}_s"].reshape(-1, 128).T for n in ("w1", "w2", "h1", "h2", "w3")],
                                  axis=1)
    arrays["th"] = T(w["L0_attn_W_theta"])
    arrays["pg"] = np.concatenate([T(w["L0_attn_W_phi"]), T(w["L0_attn_W_g"])], axis=1)
    arrays["wr"] = T(w["L1_ffn_Wr"])
    arrays["ae"] = rows(w["L1_ffn_A"].reshape(512, 128)).reshape(128, 4, 128)
    arrays["bt"] = rows(w["L1_ffn_Bw"].transpose(0, 2, 1).reshape(512, 128)).reshape(128, 4, 128)
    order = np.arange(128).reshape(4, 4, 8).transpose(1, 2, 0).reshape(-1)
    q, k = w["L1_attn_W_Q"], w["L1_attn_W_K"]
    arrays["wq"] = np.stack([q[order].T, q[order ^ 1].T, k[order].T, k[order ^ 1].T, w["L1_attn_W_V"].T], axis=1)
    arrays["wo"] = w["L1_attn_W_O"].T[order]
    f32 = np.float32
    arrays["ident"] = np.eye(128, dtype=f32)
    arrays["hident"] = np.eye(128, dtype=f32) * f32(0.5)
    arrays["mhalf"] = np.full((128, 4), -0.5, f32)
    i, j = np.arange(8)[:, None], np.arange(8)[None, :]
    arrays["tri"] = np.ascontiguousarray(np.broadcast_to((j < i).astype(f32), (128, 8, 8)))
    inv = (f32(10000.0) ** (f32(-2.0) * np.arange(4, dtype=f32) / f32(8))).astype(f32)
    ang = np.arange(S, dtype=f32)[:, None] * inv
    d = order % 8
    arrays["cos"] = np.tile(np.cos(ang).astype(f32)[:, d // 2].T, (1, 2))
    arrays["sin"] = np.tile((np.sin(ang).astype(f32)[:, d // 2] * np.where(d % 2, f32(1), f32(-1))).T, (1, 2))
    arrays = {k: np.ascontiguousarray(v) for k, v in arrays.items()}

    nc = bacc.Bacc("TRN2", target_bir_lowering=False, num_devices=1)
    I = {k: nc.dram_tensor(f"in_{k}", v.shape, mybir.dt.from_np(v.dtype), kind="ExternalInput").ap()
         for k, v in arrays.items()}
    out = nc.dram_tensor("out_0", (NB, S, D), F32, kind="ExternalOutput").ap()
    build(nc, I, out)
    r = run_bass_kernel_spmd(nc, [{f"in_{k}": v for k, v in arrays.items()}], core_ids=[0])
    return r.results[0]["out_0"]
```

```python
from contextlib import ExitStack

import numpy as np
import concourse.bass as bass
from concourse import mybir

F32 = mybir.dt.float32
F32R = mybir.dt.float32r
BF16 = mybir.dt.bfloat16
ALU = mybir.AluOpType
ACT = mybir.ActivationFunctionType
AX = mybir.AxisListType.X

NB = 16
S = 256
D = 128
HID = 512
NC = 8
TC = 512
NH = 16
DHEAD = 8
EPS = 1e-5
NEG = -1.0e30
LEAD = 7


def activation(*a, **k):
    return lambda e: e.activation(*a, **k)


def affine_select(*a, **k):
    return lambda e: e.affine_select(*a, **k)


def bn_aggr(*a, **k):
    return lambda e: e.bn_aggr(*a, **k)


def bn_stats(*a, **k):
    return lambda e: e.bn_stats(*a, **k)


def matmul(*a, **k):
    return lambda e: e.matmul(*a, **k)


def memset(*a, **k):
    return lambda e: e.memset(*a, **k)


def reciprocal(*a, **k):
    return lambda e: e.reciprocal(*a, **k)


def scalar_tensor_tensor(*a, **k):
    return lambda e: e.scalar_tensor_tensor(*a, **k)


def tensor_copy(*a, **k):
    return lambda e: e.tensor_copy(*a, **k)


def tensor_reduce(*a, **k):
    return lambda e: e.tensor_reduce(*a, **k)


def tensor_scalar(*a, **k):
    return lambda e: e.tensor_scalar(*a, **k)


def tensor_tensor(*a, **k):
    return lambda e: e.tensor_tensor(*a, **k)


def transpose(*a, **k):
    return lambda e: e.transpose(*a, **k)


class Tok:
    def __init__(self, sem, val):
        self.sem, self.val = sem, val


class Queue:

    def __init__(self, sem):
        self.sem, self.n, self.ops = sem, 0, []

    def put(self, fn, waits=(), lo=False, inc=True):
        tok = None
        if inc:
            self.n += 1
            tok = Tok(self.sem, self.n)
        self.ops.append((fn, [w for w in waits if w is not None], inc, lo))
        return tok

    def play(self, eng, lo=True, start=0, stop=None):
        seen = {}
        for fn, waits, inc, is_lo in self.ops[start:stop]:
            if is_lo and not lo:
                continue
            for w in waits:
                if seen.get(id(w.sem), 0) < w.val:
                    eng.wait_ge(w.sem, w.val)
                    seen[id(w.sem)] = w.val
            ins = fn(eng)
            if inc:
                ins.then_inc(self.sem, 1)


class Ring:

    def __init__(self, ids):
        self.ids, self.i = list(ids), -1
        self.free = {k: [] for k in self.ids}

    def take(self):
        for _ in self.ids:
            self.i = (self.i + 1) % len(self.ids)
            k = self.ids[self.i]
            if self.free[k] is not None:
                free, self.free[k] = self.free[k], None
                return k, free
        assert False, "no buffer whose last readers are issued"

    def get(self):
        while all(self.free[k] is None for k in self.ids):
            yield
        return self.take()


def build(nc, I, out):
    with ExitStack() as ctx:
        def sb(name, shape, dt=F32):
            return ctx.enter_context(nc.sbuf_tensor(name, shape, dt))

        def sem(name):
            return ctx.enter_context(nc.semaphore(name))

        X = sb("X", [128, 32, D])
        IDN = sb("IDN", [128, 128])
        HIDN = sb("HIDN", [128, 2, 128])
        IDB = sb("IDB", [128, 128], BF16)
        MKB = sb("MKB", [128, 512], BF16)
        SC = sb("SC", [128, 17])
        TH = sb("TH", [128, 32])
        PG = sb("PG", [128, 160])
        WR = sb("WR", [128, 8])
        AE = sb("AE", [128, 4, 128])
        BT = sb("BT", [128, 4, 128])
        WQ = sb("WQ", [128, 5, 128])
        WO = sb("WO", [128, 128])
        TRI = sb("TRI", [128, 2, 8, 8])
        MHALF = sb("MHALF", [128, 4])
        ST = sb("ST", [128, 4, 4, 6])
        MV = sb("MV", [128, 4, 4, 2])
        VE = sb("VE", [128, 4, 4])
        RS = sb("RS", [128, 4, 4])
        XN = sb("XN", [128, 4, 4, 128])
        XT = sb("XT", [128, 3, TC])
        LG = sb("LG", [128, 2, 2, 8])
        CP = sb("CP", [128, 2, 8, 8])
        CQ = sb("CQ", [128, 2, 8, 8])
        RK = sb("RK", [128, 2, 8])
        SM = sb("SM", [128, 4, 2, 8])
        MXS = sb("MXS", [128, 8])
        GS = sb("GS", [128, 2, 2, 4])
        GA = sb("GA", [128, 8, 128])
        WB = sb("WB", [128, 2, 2, 128])

        U = sb("U", [128, 5632])
        W5 = U
        THT = U[0:32, 0:1024].rearrange("p (a b) -> p a b", a=2)
        PH = U[:, 1024:2304].rearrange("p (a b d) -> p a b d", a=2, b=4)
        MM = U[0:32, 2304:2816].rearrange("p (a b d) -> p a b d", a=2, b=2)
        RA = [U[:, TC * n:TC * n + TC] for n in range(2)]
        CB = [U[:, TC * n:TC * n + TC].bitcast(F32R) for n in range(2, 6)]
        COS = U[:, 6 * TC:7 * TC]
        SIN = U[:, 7 * TC:8 * TC]
        XP = U[:, 8 * TC:11 * TC].rearrange("p (a b) -> p a b", a=3)

        FL = sb("FL", [128, 9])
        FS = sb("FS", [128, 10])
        FI = sb("FI", [1, 1], mybir.dt.int32)

        early = ExitStack()

        def se(name, shape, dt=F32):
            return early.enter_context(nc.sbuf_tensor(name, shape, dt))

        WH = se("WH", [128, 5632], F32R)
        WL = se("WL", [128, 5632], F32R)
        NT = 2
        fb = []
        for n in range(NT):
            fb.append({k: se(f"{k}{n}", [128, w * TC], F32R)
                       for k, w in (("xh", 1), ("xl", 1), ("ah", 4), ("al", 4), ("bh", 4), ("bl", 4))})
            fb[n]["y"] = se(f"y{n}", [128, TC])
        gbuf = [se(f"g{n}", [128, TC]) for n in range(3)]
        hbuf = [se(f"h{n}", [128, TC]) for n in range(3)]

        sems = {n: sem("s_" + n) for n in ("pe", "act", "dve", "pool", "sp")}
        pe, act, dve, pool, sp = (Queue(sems[n]) for n in ("pe", "act", "dve", "pool", "sp"))
        PSA = ctx.enter_context(nc.psum_tensor("PSA", [128, 8, 512], F32))

        def bank(i):
            return PSA[:, i, :]

        def dma(q, out_ap, in_ap, s, waits=()):
            def f(e):
                e.dma_start(out_ap, in_ap).then_inc(s, 16)
            q.ops.append((f, [w for w in waits if w is not None], False, False))

        s_w = [sem(f"s_w{i}") for i in range(6)]
        s_x = [sem(f"s_x{i}") for i in range(NC)]
        xin = I["x"].rearrange("b (c p) d -> p (b c) d", p=128)
        xout = out.rearrange("b (c p) d -> p (b c) d", p=128)
        dma(sp, X[:, 0:4, :], xin[:, 0:4, :], s_x[0])
        dma(sp, IDN[:, :], I["ident"], s_w[0])
        dma(sp, W5[:, 0:1024], I["w5"][:, 0:1024], s_w[1])
        dma(sp, SC[:, :], I["sc"], s_w[0])
        dma(sp, MHALF[:, :], I["mhalf"], s_w[0])
        t_x = [Tok(s_x[c], 16) for c in range(NC)]
        t_w0 = Tok(s_w[0], 48)
        t_w1 = Tok(s_w[1], 16)
        dma(sp, W5[:, 1024:3072], I["w5"][:, 1024:3072], s_w[2])
        dma(sp, X[:, 4:8, :], xin[:, 4:8, :], s_x[1])
        dma(sp, W5[:, 3072:5632], I["w5"][:, 3072:5632], s_w[3])
        t_w2, t_w3 = Tok(s_w[2], 16), Tok(s_w[3], 16)
        for c in range(2, NC):
            dma(sp, X[:, 4 * c:4 * c + 4, :], xin[:, 4 * c:4 * c + 4, :], s_x[c])
        n4 = 0
        for dst, src in ((TH[:, :], "th"), (PG[:, :], "pg"), (WR[:, :], "wr"), (AE[:, :, :], "ae"), (BT[:, :, :], "bt"),
                         (WQ[:, :, :], "wq"), (WO[:, :], "wo"), (TRI[:, :, :, :], "tri"), (HIDN[:, :, :], "hident")):
            dma(sp, dst, I[src], s_w[4])
            n4 += 16
        t_w4 = Tok(s_w[4], n4)

        t_c = pool.put(memset(MKB[:, :], 0.0))
        t_c = pool.put(affine_select(
            out=MKB[:, :].rearrange("p (v k) -> p v k", v=4), in_=MKB[:, :].rearrange("p (v k) -> p v k", v=4),
            compare_op=ALU.is_ge, fill=NEG, base=0, pattern=[[0, 4], [-1, 128]], channel_multiplier=1), [t_c])
        t_ib = pool.put(tensor_copy(IDB[:, :], IDN[:, :]), [t_w0])

        t_wh, t_wl = {}, {}
        parts = [(0, 1024, t_w1), (1024, 3072, t_w2), (3072, 5632, t_w3)]

        def weights(k):
            a, b, t = parts[k]
            if k == 0:
                t_wh[k] = dve.put(tensor_copy(WH[:, a:b], W5[:, a:b]), [t])
            else:
                t_wh[k] = act.put(activation(WH[:, a:b], W5[:, a:b], ACT.Copy), [t])
            q = pool if k == 2 else dve
            t_wl[k] = q.put(tensor_tensor(WL[:, a:b], W5[:, a:b], WH[:, a:b], ALU.subtract), [t_wh[k]])

        t_one = pool.put(memset(FS[:, 9:10], 1.0))
        t_fl, t_fs = [], []

        def scan(k, a, b, t):
            t_fl[:] = [act.put(activation(W5[:, a:b], WL[:, a:b].bitcast(F32), ACT.Abs, accum_out=FL[:, k:k + 1]),
                               [t])]

        def second_parts():
            t = dve.put(tensor_scalar(FS[:, 0:9], FL[:, :], 0.0, None, ALU.not_equal), t_fl)
            t_fs.append(dve.put(tensor_reduce(FL[:, 0:1], FS[:, 0:9], AX, ALU.max), [t]))

        mark = []

        def flag():
            b, free = pr.take()
            t = pe.put(matmul(PSA[0:1, b, 0:1], FL[:, 0:1], FS[:, 9:10], start=True, stop=True), t_fs + [t_one] + free)
            t = dve.put(tensor_copy(FI[:, :], PSA[0:1, b, 0:1]), [t])
            pr.free[b] = [t]
            mark.append(t)

        t_X = list(t_x)
        lnr = Ring(range(4))
        xtr = Ring(range(3))

        def layer_norm(c, q=dve):
            i, free = yield from lnr.get()
            for j in range(4):
                t = dve.put(bn_stats(ST[:, i, j, :], X[:, 4 * c + j, :]), [t_X[c]] + free)
            for j in range(4):
                ta = dve.put(bn_aggr(MV[:, i, j, :], ST[:, i, j, :]), [t])
            tv = dve.put(tensor_scalar(VE[:, i, :], MV[:, i, :, 1], EPS, None, ALU.add), [ta])
            tr = pool.put(tensor_tensor(RS[:, i, :], VE[:, i, :], MHALF[:, :], ALU.pow), [tv, t_w0])
            yield
            for j in range(4):
                tn = q.put(tensor_scalar(XN[:, i, j, :], X[:, 4 * c + j, :], MV[:, i, j, 0:1],
                                                            RS[:, i, j:j + 1], ALU.subtract, ALU.mult), [tr])
            return i, tn

        def transposes(i, tn, b, free):
            for j in range(4):
                t = pe.put(transpose(PSA[:, b, 128 * j:128 * j + 128], XN[:, i, j, :], IDN[:, :]),
                           [tn, t_w0] + free)
            lnr.free[i] = [t]
            return t

        pr = Ring(range(6))
        sr = Ring((6, 7))

        second = []

        def pause(n):
            for _ in range(n):
                yield

        def step():
            for j in list(second):
                if next(j, "end") == "end":
                    second.remove(j)

        gr = Ring(range(3))
        hr = Ring(range(3))
        last_ffn = {}
        SPL = [[(dve, dve), (dve, dve), (dve, dve), (dve, dve)],
               [(dve, dve), (act, dve), (dve, dve), (act, dve)],
               [(dve, dve), (act, dve), (dve, dve), (act, dve)]]

        def split(h, th, hi, lo, q_hi, q_lo, free):
            if q_hi is act:
                ta = act.put(activation(hi, h, ACT.Copy), [th] + free)
            else:
                ta = dve.put(tensor_copy(hi, h), [th] + free)
            tb = q_lo.put(tensor_tensor(lo, h, hi, ALU.subtract), [ta])
            return ta, tb

        def group(o, cols, hi, lo, w_hi, w_lo, ready, free):
            n = len(cols)
            for k in range(n):
                w = WH[:, cols[k]:cols[k] + 128]
                wl = WL[:, cols[k]:cols[k] + 128]
                pe.put(matmul(o, w, hi[k], start=(k == 0), stop=False), [w_hi] + ready[k] + free, inc=False)
                pe.put(matmul(o, wl, hi[k], start=False, stop=False), [w_lo], lo=True, inc=False)
                t = pe.put(matmul(o, w, lo[k], start=False, stop=(k == n - 1)), inc=(k == n - 1))
            return t

        def ffn(c, after=None):
            B = fb[c % NT]
            i, tn = yield from layer_norm(c)
            yield
            b, free = pr.take()
            tt = transposes(i, tn, b, free)
            th = act.put(activation(B["xh"][:, :], bank(b), ACT.Copy), [tt])
            tl = dve.put(tensor_tensor(B["xl"][:, :], bank(b), B["xh"][:, :], ALU.subtract), [th])
            pr.free[b] = [tl]
            yield

            def cut(name, k):
                return B[name][:, TC * k:TC * k + TC]

            ready = []
            for j in range(4):
                b1, free1 = pr.take()
                t1 = group(bank(b1), [128 * j], [B["xh"][:, :]], [B["xl"][:, :]], t_wh[0], t_wl[0], [[th, tl]], free1)
                b2, free2 = pr.take()
                t2 = group(bank(b2), [512 + 128 * j], [B["xh"][:, :]], [B["xl"][:, :]], t_wh[0], t_wl[0], [[th, tl]],
                           free2)
                if j % 2:
                    step()
                if c == 1 and j == 1 and not mark:
                    flag()
                g, gfree = gr.take()
                ta = act.put(activation(gbuf[g][:, :], bank(b1), ACT.Silu, scale=SC[:, j:j + 1]), [t1, t_w0] + gfree)
                pr.free[b1] = [ta]
                h, hfree = hr.take()
                th_ = dve.put(scalar_tensor_tensor(out=hbuf[h][:, :], in0=bank(b2), scalar=SC[:, 4 + j:5 + j],
                                                   in1=gbuf[g][:, :], op0=ALU.mult, op1=ALU.mult),
                              [t2, ta, t_w0] + hfree)
                pr.free[b2] = [th_]
                gr.free[g] = [th_]
                ready.append(list(split(hbuf[h][:, :], th_, cut("ah", j), cut("al", j), *SPL[0][j], [])))
                hr.free[h] = ready[-1]
            if len(mark) == 1:
                mark.append(len(pe.ops))
            yield
            for lay, (src, dst) in enumerate((("a", "b"), ("b", "a"))):
                k0 = 1024 + 2048 * lay
                nxt, done = [], []
                for j in range(4):
                    b1, free1 = pr.take()
                    t1 = group(bank(b1), [k0 + 512 * k + 128 * j for k in range(4)],
                               [cut(src + "h", k) for k in range(4)], [cut(src + "l", k) for k in range(4)],
                               t_wh[1 + lay], t_wl[1 + lay], ready, free1)
                    done.append(t1)
                    step()
                    h, hfree = hr.take()
                    ta = act.put(activation(hbuf[h][:, :], bank(b1), ACT.Gelu,
                                            scale=SC[:, 8 + 4 * lay + j:9 + 4 * lay + j]), [t1, t_w0] + hfree)
                    pr.free[b1] = [ta]
                    nxt.append(list(split(hbuf[h][:, :], ta, cut(dst + "h", j), cut(dst + "l", j), *SPL[1 + lay][j],
                                          [])))
                    hr.free[h] = nxt[-1]
                    if not t_fs and lay == 0:
                        scan(1 + j, 1024 + 512 * j, 1536 + 512 * j, t_wl[1])
                        scan(5 + j, 3072 + 640 * j, 3712 + 640 * j, t_wl[2])
                ready = nxt
                yield
            b1, free1 = pr.take()
            t1 = group(bank(b1), [5120 + 128 * k for k in range(4)], [cut("ah", k) for k in range(4)],
                       [cut("al", k) for k in range(4)], t_wh[2], t_wl[2], ready, free1)
            step()
            ty = act.put(activation(B["y"][:, :], bank(b1), ACT.Copy, scale=SC[:, 16:17]), [t1, t_w0])
            pr.free[b1] = [ty]
            yield
            b2, free2 = pr.take()
            for j in range(4):
                t2 = pe.put(transpose(PSA[:, b2, 128 * j:128 * j + 128], B["y"][:, 128 * j:128 * j + 128],
                                      IDN[:, :]), [ty] + free2)
            step()
            tx = dve.put(scalar_tensor_tensor(
                out=X[:, 4 * c:4 * c + 4, :].rearrange("p a d -> p (a d)"), in0=bank(b2), scalar=0.5,
                in1=X[:, 4 * c:4 * c + 4, :].rearrange("p a d -> p (a d)"), op0=ALU.mult, op1=ALU.add), [t2])
            pr.free[b2] = [tx]
            t_X[c] = tx
            last_ffn[c] = [t1, t2, tx]
            if after is not None:
                second.append(after)

        def residual(c, b, t):
            tx = dve.put(tensor_tensor(
                X[:, 4 * c:4 * c + 4, :].rearrange("p a d -> p (a d)"), bank(b),
                X[:, 4 * c:4 * c + 4, :].rearrange("p a d -> p (a d)"), ALU.add), [t])
            t_X[c] = tx
            return tx

        def normed_T(c, ring, q=dve):
            i, tn = yield from layer_norm(c, q)
            yield from pause(2)
            x, xfree = yield from xtr.get()
            b, free = yield from ring.get()
            tt = transposes(i, tn, b, free)
            te = act.put(activation(XT[:, x, :], bank(b), ACT.Copy), [tt] + xfree)
            ring.free[b] = [te]
            yield from pause(2)
            return x, te

        l0r = Ring(range(2))

        def attn0(c):
            x, te = yield from normed_T(c, sr)
            q, qfree = yield from l0r.get()
            b, free = yield from sr.get()
            t = pe.put(matmul(PSA[0:32, b, :], TH[:, :], XT[:, x, :], start=True, stop=True),
                       [te, t_w4] + free)
            t0 = act.put(activation(THT[:, q, :], PSA[0:32, b, :], ACT.Copy), [t, t_wl[2]] + t_fl + qfree)
            sr.free[b] = [t0]
            for h in range(2):
                b, free = yield from sr.get()
                for j in range(2):
                    k = 2 * h + j
                    t = pe.put(matmul(PSA[:, b, 160 * j:160 * j + 160],
                                                                 XT[:, x, 128 * k:128 * k + 128], PG[:, :],
                                                                 start=True, stop=True), [te, t_w4] + free)
                tp = act.put(activation(
                    PH[:, q, 2 * h:2 * h + 2, :].rearrange("p a d -> p (a d)"), PSA[:, b, 0:320], ACT.Copy),
                    [t] + qfree)
                sr.free[b] = [tp]
            xtr.free[x] = [t]
            yield
            b, free = yield from sr.get()
            for h in range(2):
                for j in range(2):
                    k = 2 * h + j
                    t = pe.put(matmul(PSA[0:32, b, 128 * h:128 * h + 128],
                                                                 PH[:, q, k, 0:32], PH[:, q, k, 32:160],
                                                                 start=(j == 0), stop=(j == 1)), [tp] + free)
            tm = act.put(activation(MM[:, q, :, :].rearrange("p a d -> p (a d)"), PSA[0:32, b, 0:256],
                                                ACT.Copy, scale=float(1.0 / np.sqrt(128.0))), [t] + qfree)
            sr.free[b] = [tm]
            yield
            b, free = yield from sr.get()
            for k in range(4):
                t = pe.put(matmul(PSA[:, b, 128 * k:128 * k + 128],
                                                   THT[:, q, 128 * k:128 * k + 128], MM[:, q, k // 2, :],
                                                   start=True, stop=True), [tm, t0] + free)
            l0r.free[q] = [t]
            yield
            sr.free[b] = [residual(c, b, t)]

        moer = Ring(range(2))
        small = [None]
        gar = Ring(range(1))

        def moe(c, ring, q=dve):
            x, te = yield from normed_T(c, ring, q)
            n, nfree = yield from moer.get()
            b, free = yield from ring.get()
            for h in range(2):
                t = pe.put(matmul(PSA[:, b, 8 * h:8 * h + 8], XT[:, x, 256 * h:256 * h + 1].to_broadcast([128, 128]),
                                  WR[:, :], start=True, stop=True), [te, t_w4] + free)
            yield
            L = LG[:, n, :, :]
            tl = dve.put(tensor_copy(L.rearrange("p a d -> p (a d)"), PSA[:, b, 0:16]), [t, small[0]] + nfree)
            ring.free[b] = [tl]
            Lj = L.rearrange("p h (o j) -> p h o j", o=1).to_broadcast([128, 2, 8, 8])
            Li = L.rearrange("p h (i o) -> p h i o", o=1).to_broadcast([128, 2, 8, 8])
            ta = dve.put(tensor_tensor(CP[:, :, :, :], Lj, Li, ALU.is_gt), [tl])
            tb = dve.put(tensor_tensor(CQ[:, :, :, :], Lj, Li, ALU.is_equal), [tl])
            tm = dve.put(tensor_reduce(MXS[:, 0:2], L, AX, ALU.max), [tl])
            tb = dve.put(tensor_tensor(CQ[:, :, :, :], CQ[:, :, :, :], TRI[:, :, :, :], ALU.mult), [tb])
            ts = dve.put(tensor_tensor(SM[:, 0, :, :], L,
                                       MXS[:, 0:2].rearrange("p (h o) -> p h o", o=1).to_broadcast([128, 2, 8]),
                                       ALU.subtract), [tm])
            te_ = act.put(activation(SM[:, 1, :, :], SM[:, 0, :, :], ACT.Exp), [ts])
            ta = dve.put(tensor_tensor(CP[:, :, :, :], CP[:, :, :, :], CQ[:, :, :, :], ALU.add), [tb, ta])
            tr = dve.put(tensor_reduce(RK[:, :, :], CP[:, :, :, :], AX, ALU.add), [ta])
            tk = dve.put(tensor_scalar(SM[:, 2, :, :], RK[:, :, :], 2.0, None, ALU.is_lt), [tr])
            small[0] = tk
            yield
            tk = dve.put(tensor_tensor(SM[:, 3, :, :], SM[:, 1, :, :], SM[:, 2, :, :], ALU.mult), [tk, te_])
            tz = dve.put(tensor_reduce(MXS[:, 2:4], SM[:, 3, :, :], AX, ALU.add), [tk])
            tz = dve.put(reciprocal(MXS[:, 4:6], MXS[:, 2:4]), [tz])
            for p in range(2):
                R = slice(64 * p, 64 * p + 64)
                tg = dve.put(tensor_tensor(
                    GS[R, n, :, :], SM[R, 3, :, :].rearrange("p h (c t) -> p h c t", t=2)[:, :, :, p],
                    MXS[R, 4:6].rearrange("p (h o) -> p h o", o=1).to_broadcast([64, 2, 4]), ALU.mult), [tz])
            small[0] = tg
            yield
            _, gfree = yield from gar.get()
            tga = {}
            late = c == NC - 1
            for h in range(2):
                for k in range(4):
                    q = dve if late and (h, k) not in ((0, 1), (0, 3), (1, 2)) else pool
                    tga[h, k] = q.put(tensor_scalar(GA[:, 4 * h + k, :], AE[:, k, :], GS[:, n, h, k:k + 1], 1.0,
                                                 ALU.mult, ALU.mult), [tg] + gfree)
            yield from pause(3)
            b, free = yield from ring.get()
            for h in range(2):
                for k in range(4):
                    t = pe.put(matmul(PSA[:, b, 128 * h:128 * h + 128], GA[:, 4 * h + k, :], BT[:, k, :],
                                      start=(k == 0), stop=(k == 3)), [tga[h, k]] + free)
            gar.free[0] = [t]
            yield
            tw = dve.put(scalar_tensor_tensor(
                out=WB[:, n, :, :], in0=PSA[:, b, 0:256].rearrange("p (h k) -> p h k", h=2), scalar=0.5,
                in1=HIDN[:, :, :], op0=ALU.mult, op1=ALU.add), [t])
            ring.free[b] = [tw]
            yield
            b, free = yield from ring.get()
            for k in range(4):
                t = pe.put(matmul(PSA[:, b, 128 * k:128 * k + 128], XT[:, x, 128 * k:128 * k + 128],
                                  WB[:, n, k // 2, :], start=True, stop=True), [tw] + free)
            xtr.free[x] = [t]
            moer.free[n] = [t]
            yield
            ring.free[b] = [residual(c, b, t)]

        DQ = nc.dram_tensor("dq", [NB, 4, 3, 8, 4, S], F32)
        DKK = nc.dram_tensor("dk", [NB, 4, 3, 8, 4, S], F32)
        DX = nc.dram_tensor("dx", [NC, 128, TC], F32)
        s_dq = [[sem(f"s_dq{c}"), sem(f"s_dk{c}")] for c in range(NC)]
        s_dx = [sem(f"s_dx{c}") for c in range(NC)]
        xpr = Ring(range(3))
        t_dq = {}
        rope = Ring(range(1))
        cb_free = [[], []]
        ra_free = [[]]
        s_cs = sem("s_cs")
        t_cs = Tok(s_cs, 32)

        def tables():
            for dst, src in ((COS, "cos"), (SIN, "sin")):
                dma(sp, dst, I[src], s_cs, l0r.free[0] + l0r.free[1])

        def prep(c):
            if c == 0:
                tables()
            i, tn = yield from layer_norm(c)
            yield
            x, xfree = yield from xpr.get()
            b, free = yield from sr.get()
            tt = transposes(i, tn, b, free)
            te = act.put(activation(XP[:, x, :], bank(b), ACT.Copy), [tt] + xfree + l0r.free[0] + l0r.free[1])
            sr.free[b] = [te]
            yield from pause(2)
            yield from rope.get()
            for side, dst, terms in ((1, DKK, (0, 0, 1)), (0, DQ, (0, 1, 0))):
                prods = []
                for n, tab in ((0, COS), (1, SIN)):
                    b, free = yield from sr.get()
                    t = pe.put(matmul(bank(b), WQ[:, 2 * side + n, :], XP[:, x, :], start=True, stop=True),
                               [te, t_w4] + free)
                    yield
                    tr = dve.put(tensor_tensor(RA[n], bank(b), tab, ALU.mult), [t, t_cs] + ra_free[0])
                    sr.free[b] = [tr]
                    prods.append(tr)
                ts = pool.put(tensor_tensor(RA[0], RA[0], RA[1], ALU.add), prods)
                yield
                th = dve.put(tensor_copy(CB[2 * side][:, :], RA[0]), [ts] + cb_free[side])
                yield
                tl = pool.put(tensor_tensor(CB[2 * side + 1][:, :], RA[0], CB[2 * side][:, :],
                                            ALU.subtract), [th])
                ra_free[0] = [tl]
                for m, n in enumerate(terms):
                    for u in range(2):
                        dma(sp, dst[2 * c + u, :, m].rearrange("v w g k -> v (w g) k"),
                            CB[2 * side + n][:, S * u:S * u + S].bitcast(F32), s_dq[c][side], [th, tl])
                cb_free[side] = [Tok(s_dq[c][side], 96)]
                yield
            rope.free[0] = []
            t_dq[c] = [Tok(s, 96) for s in s_dq[c]]
            dma(sp, DX[c], XP[:, x, :], s_dx[c], [te])
            xpr.free[x] = [t, Tok(s_dx[c], 16)]

        early.close()
        QS, KS, VA, OT = {}, {}, {}, {}
        for n in (2, 3):
            QS[n] = sb(f"QS{n}", [128, 4, 4, S], F32R)
        VC = sb("VC", [128, TC])
        LC = sb("LC", [128, TC])
        RC = sb("RC", [128, TC])
        ON = sb("ON", [128, TC])
        MT = sb("MT", [NH, 2, 2, S], F32R)
        for n in (0, 1):
            QS[n] = sb(f"QS{n}", [128, 4, 4, S], F32R)
        for n in range(4):
            KS[n] = sb(f"KS{n}", [128, 4, S], F32R)
        PB = [sb(f"PB{n}", [128, 1536]) for n in range(2)]
        for n in range(2):
            OT[n] = sb(f"OT{n}", [128, 4, TC])
        for n in range(4):
            VA[n] = sb(f"VA{n}", [128, 2, NH, 32])
        MX = sb("MX", [128, 2, 2, 4, 4])
        DO = nc.dram_tensor("do", [NC, 4, 32, 4, TC], F32)
        s_qs = [sem(f"s_qs{u}") for u in range(NB)]
        s_m = [sem(f"s_m{u}") for u in range(NB)]
        s_dv = [sem(f"s_dv{u}") for u in range(NB)]
        s_vl = [sem(f"s_vl{u}") for u in range(NB)]
        SCALE = float(1.0 / np.sqrt(np.float32(DHEAD)))
        dead = []
        t_qs, t_m, t_v = {}, {}, {}
        qfree = [None] * 4
        vfree = [None] * 4

        def blank(n, queues, w):
            done = []
            for v, q in zip((0, 2), queues):
                if q is act:
                    done.append(act.put(activation(
                        QS[n][:, v:v + 2, :, :].rearrange("p v g (a b) -> p (v g a) b", b=128),
                        IDN[:, :].rearrange("p (o b) -> p o b", o=1).to_broadcast([128, 16, 128]), ACT.Copy,
                        scale=0.0), w))
                else:
                    done.append(q.put(memset(QS[n][:, v:v + 2, :, :].bitcast(F32), 0.0), w))
                yield
            qfree[n] = done

        def ones(n, w):
            qfree[n] = qfree[n] + [pool.put(memset(KS[n][:, :, :].bitcast(F32), 1.0), w)]

        def opening():
            w = last_ffn[NC - 2]
            for _ in blank(0, (act, dve), w):
                pass
            ones(0, w)
            reloc(0)
            yield
            for _ in blank(1, (act, act), w):
                pass

        def reloc(u):
            w = t_dq[u // 2] + qfree[u % 4]
            qfree[u % 4] = None
            K, Q = KS[u % 4], QS[u % 4]
            dma(sp, K[0:96, :, :].bitcast(F32).rearrange("p g k -> p (g k)"),
                DKK[u].rearrange("v t w g k -> (v t w) (g k)"), s_qs[u], w)
            for v in range(4):
                dma(sp, Q[24 * v:24 * v + 24, v, :, :].bitcast(F32).rearrange("p g k -> p (g k)"),
                    DQ[u, v].rearrange("t w g k -> (t w) (g k)"), s_qs[u], w)
            t_qs[u] = Tok(s_qs[u], 5 * 16)

        def first_moe(c):
            if c == NC - 2:
                second.insert(0, opening())
            yield from moe(c, sr)
            second.append(prep(c))

        def main():
            live = []
            tasks = [ffn(c, attn0(c)) for c in range(NC)] + [ffn(c, first_moe(c)) for c in range(NC)]
            tick, n = 0, 0
            while n < len(tasks) or live:
                if tick % 2 == 0 and n < len(tasks):
                    live.insert(0, tasks[n])
                    n += 1
                for t in list(live):
                    if next(t, "end") == "end":
                        live.remove(t)
                if tick in (0, 2, 3):
                    weights({0: 0, 2: 1, 3: 2}[tick])
                if tick == 0:
                    scan(0, 0, 1024, t_wl[0])
                if tick == 4:
                    second_parts()
                tick += 1

        main()

        misc = sr

        dead.extend(last_ffn[NC - 2] + last_ffn[NC - 1])
        last_moe = [t for fl in pr.free.values() for t in fl]

        def rest():
            t = None
            while qfree[1] is None:
                yield
            for n in range(4):
                if n > 1:
                    yield from blank(n, (act, pool), dead + [t])
                    t = qfree[n][1]
                if n:
                    ones(n, dead + [t])
                    t = qfree[n][-1]
                if n == 1:
                    reloc(1)
                t = pool.put(memset(VA[n][:, :, :, 8:32], 1.0), dead + [t])
                vfree[n] = [t]
                yield

        jobs = second
        jobs.append(rest())

        def values(c):
            x, xfree = yield from xpr.get()
            dma(sp, XP[:, x, :], DX[c], s_dx[c], [Tok(s_dx[c], 16)] + xfree)
            te = Tok(s_dx[c], 32)
            yield from pause(10)
            b, free = yield from misc.get()
            for k in range(4):
                t = pe.put(matmul(PSA[:, b, 128 * k:128 * k + 128], XP[:, x, 128 * k:128 * k + 128],
                                  WQ[:, 4, :], start=True, stop=True), [te] + free)
            xpr.free[x] = [t]
            yield
            for h in range(2):
                u = 2 * c + h
                tv = act.put(activation(
                    VA[u % 4][:, :, :, 0:8],
                    PSA[:, b, 256 * h:256 * h + 256].rearrange("p (k h d) -> p k h d", k=2, h=NH), ACT.Copy),
                    [t] + vfree[u % 4] + dead)
                t_v[u] = tv
            misc.free[b] = [tv]

        t_r = [None, None]
        t_mx = {}
        mxfree = [[], []]

        def pass1(u, g):
            K, Q = KS[u % 4], QS[u % 4]
            w = [t_qs[u], t_ib] + (last_moe if u == 0 and g == 0 else [])
            for v in range(4):
                pe.put(matmul(PSA[:, 2, 128 * v:128 * v + 128], Q[0:96, v, g, 0:128],
                                               K[0:96, g, 0:128], start=(v == 0), stop=False, skip_group_check=True),
                       w + [t_r[0]], inc=False)
            ta = pe.put(matmul(PSA[:, 2, :], IDB[:, :], MKB[:, :], start=False, stop=True,
                                           skip_group_check=True))
            for p in range(2):
                for v in range(2):
                    pe.put(matmul(PSA[:, p, 256 * v:256 * v + 256],
                                                        Q[0:96, 2 * p + v, g, 128:256], K[0:96, g, :],
                                                        start=(v == 0), stop=False, skip_group_check=True),
                           w + [t_r[1]], inc=False)
                tb = pe.put(matmul(
                    PSA[:, p, :].rearrange("p (v k) -> p v k", v=2)[:, :, 128:256], IDB[:, :],
                    MKB[:, 0:256].rearrange("p (v k) -> p v k", v=2), start=False, stop=True, skip_group_check=True))
            return u, g, ta, tb

        def maxima_of(u, g, ta, tb):
            t_r[0] = dve.put(tensor_reduce(
                MX[:, u % 2, 0, :, g], PSA[:, 2, :].rearrange("p (v k) -> p v k", v=4), AX, ALU.max),
                [ta] + mxfree[u % 2])
            t_r[1] = dve.put(tensor_reduce(
                MX[:, u % 2, 1, :, g],
                PSA[:, 0:2, :].rearrange("p b (v k) -> p (b v) k", v=2), AX, ALU.max), [tb])
            if g == 3:
                jobs.insert(0, maxima(u, [t_r[0], t_r[1]]))

        def maxima(u, tr):
            yield
            b, free = yield from misc.get()
            for k in range(2):
                t = pe.put(transpose(PSA[0:NH, b, 128 * k:128 * k + 128],
                                     MX[:, u % 2, k, :, :].rearrange("p v g -> p (v g)"), IDN[:, :]), tr + free)
            mxfree[u % 2] = [t]
            th = dve.put(tensor_scalar(MT[:, u % 2, 0, :], PSA[0:NH, b, 0:256], -1.0, None, ALU.mult),
                         [t, Tok(s_m[u - 2], 32) if u >= 2 else None])
            tl = dve.put(scalar_tensor_tensor(
                out=MT[:, u % 2, 1, :], in0=PSA[0:NH, b, 0:256], scalar=-1.0, in1=MT[:, u % 2, 0, :],
                op0=ALU.mult, op1=ALU.subtract), [th])
            misc.free[b] = [tl]
            for k in range(2):
                dma(sp, QS[u % 4][96 + k:97 + k, :, :, :].bitcast(F32).rearrange("o v g k -> o (v g) k"),
                    MT[:, u % 2, k, :].bitcast(F32), s_m[u], [th, tl])
            t_m[u] = Tok(s_m[u], 32)

        t_e = [None, None]
        t_pb = {}
        pbfree = [[], []]
        nslot = [0]
        otfree = [[]] * 4
        t_ot = {}

        def pass2(u, g):
            K, Q = KS[u % 4], QS[u % 4]
            w = [t_m[u]] + (last_moe if u == 0 and g == 0 else [])
            for v in range(4):
                t = pe.put(matmul(PSA[:, 3 + v // 2, 256 * (v % 2):256 * (v % 2) + 256], K[:, g, 0:128],
                                  Q[:, v, g, :], start=(v % 2 == 0), stop=True, skip_group_check=True),
                           w + [t_e[0]], inc=(v == 3))
            t1 = pe.put(matmul(PSA[:, 5, :], K[:, g, 128:256], Q[:, :, g, 128:256], start=True, stop=True),
                        w + [t_e[1]])
            if g == 3:
                qfree[u % 4] = [t1]
            p = (4 * u + g) % 2
            te = act.put(activation(PB[p][:, 0:1024], PSA[:, 3:5, :].rearrange("p a b -> p (a b)"), ACT.Exp,
                                    scale=SCALE), [t] + pbfree[p] + dead)
            te1 = act.put(activation(PB[p][:, 1024:1536], PSA[:, 5, :], ACT.Exp, scale=SCALE), [t1])
            t_e[0], t_e[1] = te, te1
            pool.put(affine_select(
                out=PB[p][:, 0:1024].rearrange("p (v q) -> p v q", v=4)[:, :, 0:128],
                in_=PB[p][:, 0:1024].rearrange("p (v q) -> p v q", v=4)[:, :, 0:128],
                compare_op=ALU.is_ge, fill=0.0, base=0, pattern=[[0, 4], [1, 128]], channel_multiplier=-1), [te])
            t_pb[4 * u + g] = pool.put(affine_select(
                out=PB[p][:, 1024:1536].rearrange("p (v q) -> p v q", v=4),
                in_=PB[p][:, 1024:1536].rearrange("p (v q) -> p v q", v=4),
                compare_op=ALU.is_ge, fill=0.0, base=0, pattern=[[0, 4], [1, 128]], channel_multiplier=-1), [te1])

        def weigh(u, g):
            p = (4 * u + g) % 2
            c, h = divmod(u, 2)
            b, free = 7, sr.free[7]
            V = VA[u % 4]
            for v in range(4):
                pe.put(matmul(PSA[32 * v:32 * v + 32, b, 0:256], V[:, 0, 4 * g + v, :],
                                               PB[p][:, 256 * v:256 * v + 256], start=True, stop=False),
                       [t_pb[4 * u + g], t_v[u], t_v[2 * c + 1]] + free, inc=False)
            for v in range(4):
                t = pe.put(matmul(PSA[32 * v:32 * v + 32, b, 128:256], V[:, 1, 4 * g + v, :],
                                                   PB[p][:, 1024 + 128 * v:1152 + 128 * v], start=False, stop=True))
            pbfree[p] = [t]
            if g == 3:
                vfree[u % 4] = [t]
            to = act.put(activation(OT[c % 2][:, g, S * h:S * h + S], PSA[:, b, 0:256], ACT.Copy),
                         [t] + otfree[u % 4] + dead)
            misc.free[b] = [to]
            t_ot[c] = to

        vcfree = {0: [], 1: []}
        onfree = {0: [], 1: []}
        t_on = {}

        def fin(c, u, n):
            h = u % 2
            hs = slice(S * h, S * h + S * n)
            last = u + n == 2 * c + 2
            dma(sp, DO[c].rearrange("v r g t -> (v r) g t")[:, :, hs], OT[c % 2][:, :, hs], s_dv[u], [t_ot[c]])
            td = Tok(s_dv[u], 16)
            for m in range(u, u + n):
                otfree[m % 4] = [td]
            yield from pause(2)
            halves = [m % 2 for m in range(u, u + n)]
            while any(vcfree[m] is None for m in halves):
                yield
            w = [t for m in halves for t in vcfree[m]] + dead
            for m in halves:
                vcfree[m] = None
            for T, r in ((VC, 0), (LC, 8)):
                dma(sp, T[:, hs], DO[c, :, r:r + 8, :, hs].rearrange("v r g t -> v (r g) t"), s_vl[u],
                    [td] + w)
            yield from pause(5)
            for k in range(2 * n):
                ks = slice(S * h + 128 * k, S * h + 128 * k + 128)
                tr = dve.put(reciprocal(RC[:, ks], LC[:, ks]), [Tok(s_vl[u], 32)] + w)
                yield
            while any(onfree[m] is None for m in halves):
                yield
            t_on[u] = pool.put(tensor_tensor(ON[:, hs], VC[:, hs], RC[:, hs], ALU.mult), [tr] + [t for m in halves for t in onfree[m]])
            for m in halves:
                t_on[2 * c + m] = t_on[u]
                vcfree[m] = [t_on[u]]
                onfree[m] = None
            if not last:
                return
            yield from pause(2)
            b, free = yield from misc.get()
            for k in range(4):
                t = pe.put(matmul(PSA[:, b, 128 * k:128 * k + 128], ON[:, 128 * k:128 * k + 128], WO[:, :],
                                  start=True, stop=True), [t_on[2 * c], t_on[2 * c + 1]] + free)
            onfree[0] = onfree[1] = [t]
            misc.free[b] = [residual(c, b, t)]
            yield
            yield from moe(c, sr)
            dma(sp, xout[:, 4 * c:4 * c + 4, :], X[:, 4 * c:4 * c + 4, :], s_out, [t_X[c]])

        s_out = sem("s_out")
        for s in range(-1, 4 * NB + LEAD + 2):
            if (s + 5) % 4 == 0 and 1 < (s + 5) // 4 < NB:
                reloc((s + 5) // 4)
            if (s % 8 == 5 or s == -1) and (s + 3) // 8 < NC:
                jobs.insert(0, values((s + 3) // 8))
            if s == LEAD - 1:
                sr.ids.remove(7)
            reduces = None
            if 0 <= s < 4 * NB:
                reduces = pass1(s // 4, s % 4)
            step()
            if reduces is not None:
                maxima_of(*reduces)
            k = s - LEAD
            if 0 <= k < 4 * NB:
                pass2(k // 4, k % 4)
            step()
            k -= 1
            if 0 <= k < 4 * NB:
                weigh(k // 4, k % 4)
                if k // 8 == NC - 1 and k % 4 == 3:
                    jobs.append(fin(k // 8, k // 4, 1))
                elif k % 8 == 7:
                    jobs.append(fin(k // 8, k // 4 - 1, 2))
        while jobs:
            step()

        def end(e):
            e.wait_ge(s_out, 16 * NC)
        sp.ops.append((end, [], False, False))


        block = ctx.enter_context(nc.Block())

        @block.sync
        def _(e):
            sp.play(e)

        @block.tensor
        def _(e):
            pe.play(e, stop=mark[1])
            e.wait_ge(mark[0].sem, mark[0].val)
            some = e.value_load(FI[0:1, 0:1], min_val=0, max_val=128)
            with e.If(some > 0):
                pe.play(e, start=mark[1])
            with e.Else():
                pe.play(e, lo=False, start=mark[1])

        @block.vector
        def _(e):
            dve.play(e)

        @block.scalar
        def _(e):
            act.play(e)

        @block.gpsimd
        def _(e):
            pool.play(e)


def kernel(**inputs):
    import concourse.bacc as bacc
    from concourse.bass_utils import run_bass_kernel_spmd

    w = {k: np.ascontiguousarray(v) for k, v in inputs.items()}
    T = lambda a: np.ascontiguousarray(a.T)

    def rows(a):
        return np.ascontiguousarray(a.reshape(-1, 128, a.shape[1]).transpose(1, 0, 2).reshape(128, -1))

    arrays = {"x": w["L0_attn_x"]}
    arrays["w5"] = np.concatenate([T(w["L0_ffn_w1_w"]), T(w["L0_ffn_w2_w"]), rows(T(w["L0_ffn_h1_w"])),
                                   rows(T(w["L0_ffn_h2_w"])), rows(T(w["L0_ffn_w3_w"]))], axis=1)
    arrays["sc"] = np.concatenate([w[f"L0_ffn_{n}_s"].reshape(-1, 128).T for n in ("w1", "w2", "h1", "h2", "w3")],
                                  axis=1)
    arrays["th"] = T(w["L0_attn_W_theta"])
    arrays["pg"] = np.concatenate([T(w["L0_attn_W_phi"]), T(w["L0_attn_W_g"])], axis=1)
    arrays["wr"] = T(w["L1_ffn_Wr"])
    arrays["ae"] = rows(w["L1_ffn_A"].reshape(512, 128)).reshape(128, 4, 128)
    arrays["bt"] = rows(w["L1_ffn_Bw"].transpose(0, 2, 1).reshape(512, 128)).reshape(128, 4, 128)
    order = np.arange(128).reshape(4, 4, 8).transpose(1, 2, 0).reshape(-1)
    q, k = w["L1_attn_W_Q"], w["L1_attn_W_K"]
    arrays["wq"] = np.stack([q[order].T, q[order ^ 1].T, k[order].T, k[order ^ 1].T, w["L1_attn_W_V"].T], axis=1)
    arrays["wo"] = w["L1_attn_W_O"].T[order]
    f32 = np.float32
    arrays["ident"] = np.eye(128, dtype=f32)
    arrays["hident"] = np.stack([np.eye(128, dtype=f32) * f32(0.5)] * 2, axis=1)
    arrays["mhalf"] = np.full((128, 4), -0.5, f32)
    i, j = np.arange(8)[:, None], np.arange(8)[None, :]
    arrays["tri"] = np.ascontiguousarray(np.broadcast_to((j < i).astype(f32), (128, 2, 8, 8)))
    inv = (f32(10000.0) ** (f32(-2.0) * np.arange(4, dtype=f32) / f32(8))).astype(f32)
    ang = np.arange(S, dtype=f32)[:, None] * inv
    d = order % 8
    arrays["cos"] = np.tile(np.cos(ang).astype(f32)[:, d // 2].T, (1, 2))
    arrays["sin"] = np.tile((np.sin(ang).astype(f32)[:, d // 2] * np.where(d % 2, f32(1), f32(-1))).T, (1, 2))
    arrays = {k: np.ascontiguousarray(v) for k, v in arrays.items()}

    nc = bacc.Bacc("TRN2", target_bir_lowering=False, num_devices=1)
    I = {k: nc.dram_tensor(f"in_{k}", v.shape, mybir.dt.from_np(v.dtype), kind="ExternalInput").ap()
         for k, v in arrays.items()}
    out = nc.dram_tensor("out_0", (NB, S, D), F32, kind="ExternalOutput").ap()
    build(nc, I, out)
    r = run_bass_kernel_spmd(nc, [{f"in_{k}": v for k, v in arrays.items()}], core_ids=[0])
    return r.results[0]["out_0"]
```
